# Optimizing a Trainium2 kernel written in Bass

```python
import numpy as np
import jax
import jax.numpy as jnp

def _softmax(x, axis=-1):
    return jax.nn.softmax(x, axis=axis)

def _gelu(x):
    return jax.nn.gelu(x, approximate=True)

def _silu(x):
    return jax.nn.silu(x)

def _sigmoid(x):
    return jax.nn.sigmoid(x)

def _layernorm(x, axis=-1, eps=1e-05):
    m = jnp.mean(x, axis=axis, keepdims=True)
    v = jnp.var(x, axis=axis, keepdims=True)
    return (x - m) / jnp.sqrt(v + eps)

def _scatter_add(tgt, idx, src, axis=0):
    return tgt.at[idx].add(src)

def _segment_sum(src, seg, n):
    return jax.ops.segment_sum(src, seg, n)
kernel_name = 'mk_gnn_preln_d1_gnn_r8_bc9461'

def setup_inputs(seed: int=0):
    np.random.seed(seed)
    _w = jnp.asarray

    def _rec_inputs():
        import jax
        import jax.numpy as jnp
        _gk = jax.random.key(seed)
        x = -0.0003713 + 1 * jax.random.normal(jax.random.fold_in(_gk, 1), (12500, 128), jnp.float32)
        src = jax.random.randint(jax.random.fold_in(_gk, 2), (400000,), 0, 12500, jnp.int32)
        dst = jnp.minimum((12500 * jax.random.uniform(jax.random.fold_in(_gk, 3), (400000,)) ** 2.0).astype(jnp.int32), 99999)
        _o = jnp.argsort(dst, stable=True)
        src = src[_o]
        dst = dst[_o]
        return (x, src, dst)
    x, src, dst = _rec_inputs()

    def _L0_gnn_setup():
        import jax, jax.numpy as jnp
        import numpy as np
        N = 12500
        E = 75000
        D_IN = 128
        D = 128
        L = 3

        def gru_cell(m, h, w_ih, w_hh, b_ih, b_hh):
            gi = m @ w_ih.T + b_ih
            gh = h @ w_hh.T + b_hh
            ir, iz, inn = jnp.split(gi, 3, axis=-1)
            hr, hz, hn = jnp.split(gh, 3, axis=-1)
            r = jax.nn.sigmoid(ir + hr)
            z = jax.nn.sigmoid(iz + hz)
            n = jnp.tanh(inn + r * hn)
            return (1.0 - z) * n + z * h
        key = jax.random.key(seed)
        ks = jax.random.split(key, 10)
        s = 1.0 / np.sqrt(D)
        x = jax.random.normal(ks[0], (N, D_IN), dtype=jnp.float32)
        edge_index = jax.random.randint(ks[1], (2, E), 0, N, dtype=jnp.int64)
        lin_w = jax.random.normal(ks[2], (D, D_IN), dtype=jnp.float32) * (1.0 / np.sqrt(D_IN))
        lin_b = jnp.zeros((D,), dtype=jnp.float32)
        weight = jax.random.normal(ks[3], (L, D, D), dtype=jnp.float32) * s
        w_ih = jax.random.normal(ks[4], (3 * D, D), dtype=jnp.float32) * s
        w_hh = jax.random.normal(ks[5], (3 * D, D), dtype=jnp.float32) * s
        b_ih = jnp.zeros((3 * D,), dtype=jnp.float32)
        b_hh = jnp.zeros((3 * D,), dtype=jnp.float32)
        return {'x': x, 'lin_w': lin_w, 'lin_b': lin_b, 'weight': weight, 'w_ih': w_ih, 'w_hh': w_hh, 'b_ih': b_ih, 'b_hh': b_hh, 'edge_index': edge_index}
    _L0_gnn_all = _L0_gnn_setup()
    _L0_gnn_in = {k: v for k, v in _L0_gnn_all.items() if k in ('lin_w', 'lin_b', 'weight', 'w_ih', 'w_hh', 'b_ih', 'b_hh')}
    del _L0_gnn_all
    return {'x': x, 'src': src, 'dst': dst, 'L0_gnn_lin_w': _L0_gnn_in['lin_w'], 'L0_gnn_lin_b': _L0_gnn_in['lin_b'], 'L0_gnn_weight': _L0_gnn_in['weight'], 'L0_gnn_w_ih': _L0_gnn_in['w_ih'], 'L0_gnn_w_hh': _L0_gnn_in['w_hh'], 'L0_gnn_b_ih': _L0_gnn_in['b_ih'], 'L0_gnn_b_hh': _L0_gnn_in['b_hh']}

def reference(x, src, dst, L0_gnn_lin_w, L0_gnn_lin_b, L0_gnn_weight, L0_gnn_w_ih, L0_gnn_w_hh, L0_gnn_b_ih, L0_gnn_b_hh):
    import jax
    import jax.numpy as jnp

    def _L0_gnn_ref(x, lin_w, lin_b, weight, w_ih, w_hh, b_ih, b_hh, edge_index):
        import jax, jax.numpy as jnp
        import numpy as np
        N = 12500
        E = 75000
        D_IN = 128
        D = 128
        L = 3

        def gru_cell(m, h, w_ih, w_hh, b_ih, b_hh):
            gi = m @ w_ih.T + b_ih
            gh = h @ w_hh.T + b_hh
            ir, iz, inn = jnp.split(gi, 3, axis=-1)
            hr, hz, hn = jnp.split(gh, 3, axis=-1)
            r = jax.nn.sigmoid(ir + hr)
            z = jax.nn.sigmoid(iz + hz)
            n = jnp.tanh(inn + r * hn)
            return (1.0 - z) * n + z * h
        h = x @ lin_w.T + lin_b
        src, dst = (edge_index[0], edge_index[1])
        n_nodes = h.shape[0]
        for i in range(weight.shape[0]):
            m = h @ weight[i]
            agg = jax.ops.segment_sum(m[src], dst, num_segments=n_nodes)
            h = gru_cell(agg, h, w_ih, w_hh, b_ih, b_hh)
        return h
    edge_index = jnp.stack([src, dst])
    h = jnp.maximum(_layernorm(x, axis=-1), 0.0)
    x = x + _L0_gnn_ref(h, L0_gnn_lin_w, L0_gnn_lin_b, L0_gnn_weight, L0_gnn_w_ih, L0_gnn_w_hh, L0_gnn_b_ih, L0_gnn_b_hh, edge_index)
    return x

_drawn_inputs = setup_inputs


def setup_inputs(seed=0):
    import zlib

    import numpy as np

    out = dict(_drawn_inputs(seed))
    spreads = {'L0_gnn_lin_b': (0.0, 0.1), 'L0_gnn_b_ih': (0.0, 0.1), 'L0_gnn_b_hh': (0.0, 0.1)}
    factors = {}
    for name, (base, spread) in spreads.items():
        noise = np.random.default_rng([zlib.crc32(name.encode()), seed]).standard_normal(out[name].shape)
        drawn = base * np.exp(spread * noise) if base else spread * noise
        out[name] = jnp.asarray(drawn.astype(out[name].dtype))
    for name, factor in factors.items():
        out[name] = (out[name] * factor).astype(out[name].dtype)
    return out
```

```python
import concourse.bass as bass
from concourse import mybir
from contextlib import ExitStack


def build(nc, x, src, dst, lin_wT, lin_b, weightT, w_ihT, w_hhT, b_ih, b_hh, out, NODES, EDGES, LAYERS):
    fp32 = mybir.dt.float32
    i32 = mybir.dt.int32
    ALU = mybir.AluOpType
    ACT = mybir.ActivationFunctionType
    AX = mybir.AxisListType

    P = 128
    TILES = EDGES // P
    TG = 5
    GROUPS = TILES // TG
    SLOTS = 5
    GITER = GROUPS // SLOTS
    QR = 125
    TQ = TILES // QR
    WIN = 128
    SWIN = 512
    CH = 500
    CP = 125
    CJ = CH // CP
    CHUNKS = NODES // CH
    CITER = CHUNKS // SLOTS
    SWINS = -(-NODES // SWIN)
    AGGW = max(SWINS * SWIN, NODES + WIN, 4 * TQ * P)
    EPS = 1e-5
    assert TILES * P == EDGES and GITER * SLOTS * TG == TILES and TQ * QR == TILES
    assert CITER * SLOTS * CH == NODES and TQ % TG == 0

    ctx = ExitStack()
    with ctx:
        def sb(name, shape, dt=fp32):
            return ctx.enter_context(nc.sbuf_tensor(name, shape, dt))

        def sem(name):
            return ctx.enter_context(nc.semaphore(name))

        table = nc.dram_tensor("table", [NODES, P], fp32, kind="Internal").ap()
        bases_dram = nc.dram_tensor("bases_dram", [QR, TQ // TG], i32, kind="Internal").ap()

        aggT = sb("aggT", [P, AGGW])
        stateT = sb("stateT", [P, NODES])
        srcT = sb("srcT", [P, TILES], i32)
        relT = sb("relT", [P, TILES])
        dstT = sb("dstT", [P, TILES])
        rows = sb("rows", [P, SLOTS, TG, P])
        onehot = sb("onehot", [P, SLOTS, TG * P])
        onehot_slow = onehot[:, 0:4, :].rearrange("p s n -> p (s n)").rearrange("p (t n) -> p t n", n=SWIN)
        idx = sb("idx", [P, SLOTS, TG], i32)
        shifted = sb("shifted", [P, TG])
        iota_i = sb("iota_i", [P, SWIN], i32)
        iota_f = sb("iota_f", [P, SWIN])
        ident = sb("ident", [P, P])
        bases = sb("bases", [1, GROUPS], i32)
        wide_i = sb("wide_i", [1, 1], i32)
        lo = sb("lo", [QR, TQ // TG])
        hi = sb("hi", [QR, TQ // TG])
        span = sb("span", [QR, 1])
        lo_i = sb("lo_i", [QR, TQ // TG], i32)
        widest = sb("widest", [1, 1])

        lin_sb = sb("lin_sb", [P, P])
        wT_sb = sb("wT_sb", [P, LAYERS, P])
        wih_sb = sb("wih_sb", [P, 3 * P])
        whh_sb = sb("whh_sb", [P, 3 * P])
        comb = sb("comb", [P, LAYERS, 3 * P])
        lin_bias = sb("lin_bias", [P, 1])
        bih = sb("bih", [P, 3])
        bhh = sb("bhh", [P, 3])
        brz = sb("brz", [P, 2])
        eps_t = sb("eps_t", [P, 1])

        xrow = sb("xrow", [CP, SLOTS, CJ * P])
        hrow = sb("hrow", [CP, SLOTS, CJ * P])
        stats = sb("stats", [CP, CJ, 6])
        mv = sb("mv", [CP, CJ, 2])
        rstd = sb("rstd", [CP, CJ])
        xn = sb("xn", [CP, CJ * P])
        lnT = sb("lnT", [P, CH])
        spare = onehot[:, :, :].rearrange("p s n -> p (s n)")
        gr, gz, npre, cand, diff = (spare[:, i * CH:(i + 1) * CH] for i in range(5))
        hnew = sb("hnew", [P, CH])

        bank = [ctx.enter_context(nc.psum_tensor(f"bank{i}", [P, 512], fp32)) for i in range(8)]
        ps_r, ps_z, ps_in, ps_hn, ps_rows, ps_ln, ps_lin, ps_misc = bank

        EW = TQ * P
        src_rows = aggT[0:QR, 0:EW].bitcast(i32)
        dst_rows = aggT[0:QR, EW:2 * EW].bitcast(i32)
        dst_f = aggT[0:QR, 2 * EW:3 * EW]
        rel_f = aggT[0:QR, 3 * EW:4 * EW]
        srcT_g = srcT[:, :].rearrange("p (q g) -> p g q", g=TQ)
        dstT_g = dstT[:, :].rearrange("p (q g) -> p g q", g=TQ)
        relT_g = relT[:, :].rearrange("p (q g) -> p g q", g=TQ)

        s_src = sem("src_loaded")
        s_dst = sem("dst_loaded")
        s_w = sem("weights_loaded")
        s_const = sem("constants_ready")
        s_iota = sem("iota_written")
        s_dve = sem("dve_setup_step")
        s_srcf = sem("src_as_float")
        s_dstf = sem("dst_as_float")
        s_rel = sem("rel_ready")
        s_lo_st = sem("bases_stored")
        s_bases = sem("bases_loaded")
        s_lo = sem("bases_int_ready")
        s_span = sem("span_ready")
        s_spanT = sem("span_transposed")
        s_wide = sem("wide_flag_ready")
        s_eT = sem("edges_transposed")
        s_eC = sem("edges_copied")
        s_comb = sem("combined_product")
        s_combC = sem("combined_copied")
        s_xload = [sem(f"x_loaded{k}") for k in range(SLOTS)]
        s_xused = sem("x_used")
        s_stats = sem("ln_step")
        s_var = sem("variance_ready")
        s_std = sem("std_ready")
        s_xn = sem("x_normed")
        s_lnT = sem("ln_transposed")
        s_lnC = sem("ln_copied")
        s_lin = sem("linear_product")
        s_h0 = sem("state_written")
        s_keep = sem("state_kept")
        s_rT = sem("rows_transposed")
        s_rC = sem("rows_staged")
        s_rS = [sem(f"rows_stored{k}") for k in range(SLOTS)]
        s_idx = sem("indices_ready")
        s_got = [sem(f"rows_gathered{k}") for k in range(SLOTS)]
        s_sum = sem("group_summed")
        s_taken = sem("sums_taken")
        s_oh = sem("onehot_ready")
        s_zero = sem("agg_zeroed")
        s_agg = sem("layer_aggregated")
        s_sh = sem("slow_shifted")
        s_slow_oh = sem("slow_onehot_ready")
        s_slow_sum = sem("slow_window_summed")
        s_slow_add = sem("slow_window_added")
        s_rz = sem("rz_product")
        s_n = sem("n_product")
        s_rzread = sem("gates_ready")
        s_nread = sem("n_pre_ready")
        s_t1 = sem("reset_applied")
        s_cand = sem("candidate_ready")
        s_d = sem("update_step")
        s_passed = sem("wait_passed")

        def chunk_rows(t, c):
            return t.rearrange("(c p j) f -> p c (j f)", p=CP, j=CJ)[:, bass.ds(c, 1), :].rearrange("p o n -> p (o n)")

        def wait_past(eng, semaphore, value):
            if isinstance(value, int) and value == 0:
                return
            eng.wait_ge(semaphore, value)

        def iterations(eng, count, body, peel):
            if peel:
                body(0)
            with eng.Fori(1 if peel else 0, count) as it:
                body(it)

        with nc.Block() as block:

            @block.sync
            def _(sp):
                sp.dma_start(dst_rows, dst.rearrange("(q n) -> q n", q=QR)).then_inc(s_dst, 16)
                sp.dma_start(src_rows, src.rearrange("(q n) -> q n", q=QR)).then_inc(s_src, 16)
                sp.dma_start(wT_sb[:, :, :], weightT.rearrange("l k f -> k l f")).then_inc(s_w, 16)
                sp.dma_start(wih_sb[:, :], w_ihT).then_inc(s_w, 16)
                sp.dma_start(whh_sb[:, :], w_hhT).then_inc(s_w, 16)
                sp.dma_start(lin_sb[:, :], lin_wT).then_inc(s_w, 16)
                with nc.allow_non_contiguous_dma(reason="biases, one per partition"):
                    sp.dma_start(lin_bias[:, :], lin_b.rearrange("(p o) -> p o", o=1)).then_inc(s_w, 16)
                    sp.dma_start(bih[:, :], b_ih.rearrange("(g p) -> p g", p=P)).then_inc(s_w, 16)
                    sp.dma_start(bhh[:, :], b_hh.rearrange("(g p) -> p g", p=P)).then_inc(s_w, 16)
                sp.wait_ge(s_lo, 1)
                sp.dma_start(bases_dram, lo_i[:, :]).then_inc(s_lo_st, 16)
                sp.wait_ge(s_lo_st, 16)
                sp.dma_start(bases[:, :], bases_dram.rearrange("(o q) g -> o (q g)", o=1)).then_inc(s_bases, 16)

                def store_rows(stage, target):
                    with sp.Fori(0, CITER) as it:
                        for k in range(SLOTS):
                            c = it * SLOTS + k
                            sp.wait_ge(s_rC, c + stage * CHUNKS + 1)
                            sp.dma_start(chunk_rows(target, c), hrow[:, k, :]).then_inc(s_rS[k], 16)

                for stage in range(LAYERS):
                    store_rows(stage, table)
                store_rows(LAYERS, out)
                for k in range(SLOTS):
                    sp.wait_ge(s_rS[k], 16 * CITER * (LAYERS + 1))

            @block.gpsimd
            def _(pool):
                nc.gpsimd.iota(iota_i[:, :], pattern=[[1, SWIN]], base=0, channel_multiplier=0).then_inc(s_iota, 1)
                nc.gpsimd.memset(ident[:, :], 0.0).then_inc(s_iota, 1)
                nc.gpsimd.memset(eps_t[:, :], EPS).then_inc(s_iota, 1)
                pool.wait_ge(s_iota, 3)
                nc.gpsimd.tensor_copy(iota_f[:, :], iota_i[:, :]).then_inc(s_const, 1)
                nc.gpsimd.affine_select(out=ident[:, :], in_=ident[:, :], compare_op=ALU.not_equal, fill=1.0, base=0,
                                        pattern=[[-1, P]], channel_multiplier=1).then_inc(s_const, 1)

                def load_x(uses):
                    with pool.Fori(0, CITER) as it:
                        for k in range(SLOTS):
                            c = it * SLOTS + k
                            pool.wait_ge(s_xused, c + uses * CHUNKS + 1)
                            pool.dma_start(xrow[:, k, :], chunk_rows(x, c)).then_inc(s_xload[k], 16)

                load_x(0)
                for layer in range(LAYERS):
                    for k in range(SLOTS):
                        pool.wait_ge(s_rS[k], 16 * CITER * (layer + 1))
                    with pool.Fori(0, GITER) as it:
                        for k in range(SLOTS):
                            n = it * SLOTS + (k + layer * GROUPS)
                            pool.wait_ge(s_idx, n + 1)
                            pool.wait_ge(s_sum, n + 1)
                            pool.sem_inc(s_passed, 1)
                            for j in range(TG):
                                pool.indirect_dma_start(
                                    rows[:, k, j, :], None, table,
                                    bass.IndirectOffsetOnAxis(ap=idx[:, k, j:j + 1], axis=0)).then_inc(s_got[k], 16)
                load_x(1)

            @block.tensor
            def _(pe):
                pe.sem_inc(s_sum, SLOTS)
                pe.wait_ge(s_const, 2)

                n = 0
                for what, ready in ((dst_f, s_dstf), (rel_f, s_rel), (src_rows.bitcast(fp32), s_srcf)):
                    pe.wait_ge(ready, 1)
                    for g in range(TQ):
                        if n >= 2:
                            pe.wait_ge(s_eC, n - 1)
                        nc.tensor.transpose(bank[n % 2][:, 0:QR], what[:, g * P:(g + 1) * P],
                                            ident[0:QR, 0:QR]).then_inc(s_eT, 1)
                        n += 1
                pe.wait_ge(s_span, 1)
                nc.tensor.transpose(ps_misc[0:1, 0:QR], span[:, :], ident[0:QR, 0:QR]).then_inc(s_spanT, 1)

                pe.wait_ge(s_w, 16 * 7)
                pe.wait_ge(s_eC, n)
                for layer in range(LAYERS):
                    nc.tensor.matmul(bank[layer][:, 0:3 * P], wT_sb[:, layer, :], wih_sb[:, :], start=True,
                                     stop=True).then_inc(s_comb, 1)

                def transpose_rows(u):
                    pe.wait_ge(s_h0, u + 1)
                    wait_past(pe, s_rC, u)
                    for j in range(CJ):
                        t = nc.tensor.transpose(
                            ps_rows[0:CP, j * P:(j + 1) * P],
                            hnew[:, bass.ds(j, CP, CJ)], ident[:, :])
                    t.then_inc(s_rT, 1)

                def linear_step(it):
                    for k in range(SLOTS):
                        c = it * SLOTS + k
                        pe.wait_ge(s_xn, c + 1)
                        wait_past(pe, s_lnC, c)
                        for j in range(CJ):
                            t = nc.tensor.transpose(ps_ln[:, j * CP:(j + 1) * CP], xn[:, j * P:(j + 1) * P],
                                                    ident[0:CP, 0:CP])
                        t.then_inc(s_lnT, 1)
                        pe.wait_ge(s_lnC, c + 1)
                        wait_past(pe, s_h0, c)
                        nc.tensor.matmul(ps_lin[:, 0:CH], lin_sb[:, :], lnT[:, :], start=True,
                                         stop=True).then_inc(s_lin, 1)
                        transpose_rows(c)

                iterations(pe, CITER, linear_step, peel=True)
                pe.wait_ge(s_combC, 1)
                pe.wait_ge(s_bases, 16)
                pe.wait_ge(s_wide, 1)
                wide = pe.value_load(wide_i[0:1, 0:1], min_val=0, max_val=1)

                for layer in range(LAYERS):
                    with pe.If(wide):
                        with pe.Fori(0, GITER) as it:
                            for k in range(SLOTS):
                                n = it * SLOTS + (k + layer * GROUPS)
                                pe.wait_ge(s_got[k], (it + (layer * GITER + 1)) * (16 * TG))
                                pe.sem_inc(s_passed, 1)
                                with pe.Fori(0, SWINS) as w:
                                    pe.wait_ge(s_slow_oh, n * SWINS + w + 1)
                                    for j in range(TG):
                                        t = nc.tensor.matmul(bank[0][:, 0:SWIN], rows[:, k, j, :], onehot_slow[:, j, :],
                                                             start=(j == 0), stop=(j == TG - 1))
                                    t.then_inc(s_slow_sum, 1)
                                pe.wait_ge(s_slow_sum, (n + 1) * SWINS)
                                pe.sem_inc(s_sum, 1)
                    with pe.Else():
                        with pe.Fori(0, GITER) as it:
                            for k in range(SLOTS):
                                n = it * SLOTS + (k + layer * GROUPS)
                                pe.wait_ge(s_oh, n + 1)
                                pe.wait_ge(s_taken, n + 1)
                                pe.wait_ge(s_got[k], (it + (layer * GITER + 1)) * (16 * TG))
                                for j in range(TG):
                                    t = nc.tensor.matmul(bank[k][:, 0:WIN], rows[:, k, j, :],
                                                         onehot[:, k, j * P:(j + 1) * P],
                                                         start=(j == 0), stop=(j == TG - 1))
                                t.then_inc(s_sum, 1)

                    pe.wait_ge(s_agg, layer + 1)
                    pe.wait_ge(s_keep, (layer + 1) * CHUNKS)

                    def gates(c, v):
                        hc = stateT[:, bass.ds(c * CH, CH)]
                        ac = aggT[:, bass.ds(c * CH, CH)]
                        wait_past(pe, s_rzread, v)
                        for g, ps in ((0, ps_r), (1, ps_z)):
                            nc.tensor.matmul(ps[:, 0:CH], comb[:, layer, g * P:(g + 1) * P], ac, start=True, stop=False)
                            t = nc.tensor.matmul(ps[:, 0:CH], whh_sb[:, g * P:(g + 1) * P], hc, start=False, stop=True)
                        t.then_inc(s_rz, 1)
                        wait_past(pe, s_nread, v)
                        nc.tensor.matmul(ps_in[:, 0:CH], comb[:, layer, 2 * P:3 * P], ac, start=True, stop=True)
                        nc.tensor.matmul(ps_hn[:, 0:CH], whh_sb[:, 2 * P:3 * P], hc, start=True,
                                         stop=True).then_inc(s_n, 1)

                    def step(it, k, first):
                        c = it * SLOTS + k
                        gates(c, c + layer * CHUNKS)
                        if not first:
                            transpose_rows(c + ((layer + 1) * CHUNKS - 1))

                    for k in range(SLOTS):
                        step(0, k, k == 0)
                    with pe.Fori(1, CITER) as it:
                        for k in range(SLOTS):
                            step(it, k, False)
                    transpose_rows((layer + 2) * CHUNKS - 1)

            @block.scalar
            def _(act):
                n = 0
                for to in (dstT_g, relT_g, srcT_g):
                    for g in range(TQ):
                        act.wait_ge(s_eT, n + 1)
                        nc.scalar.copy(to[:, g, :], bank[n % 2][:, 0:QR]).then_inc(s_eC, 1)
                        n += 1
                for layer in range(LAYERS):
                    act.wait_ge(s_comb, layer + 1)
                    t = nc.scalar.copy(comb[:, layer, :], bank[layer][:, 0:3 * P])
                t.then_inc(s_combC, 1)

                def keep_state(c, u):
                    act.wait_ge(s_h0, u + 1)
                    nc.scalar.copy(stateT[:, bass.ds(c * CH, CH)], hnew[:, :]).then_inc(s_keep, 1)

                def stage_rows(it, k, u, stage):
                    act.wait_ge(s_rT, u + 1)
                    wait_past(act, s_rS[k], (it + stage * CITER) * 16)
                    nc.scalar.copy(hrow[:, k, :], ps_rows[0:CP, :]).then_inc(s_rC, 1)

                def linear_step(it):
                    for k in range(SLOTS):
                        c = it * SLOTS + k
                        act.wait_ge(s_var, c + 1)
                        nc.scalar.activation(rstd[:, :], mv[:, :, 1], ACT.Sqrt, bias=eps_t[0:CP, :]).then_inc(s_std, 1)
                        act.wait_ge(s_lnT, c + 1)
                        wait_past(act, s_lin, c)
                        nc.scalar.activation(lnT[:, :].rearrange("f (p j) -> f j p", j=CJ),
                                             ps_ln[:, 0:CH].rearrange("f (j p) -> f j p", j=CJ),
                                             ACT.Relu).then_inc(s_lnC, 1)
                        act.wait_ge(s_lin, c + 1)
                        wait_past(act, s_keep, c)
                        wait_past(act, s_rT, c)
                        nc.scalar.activation(hnew[:, :], ps_lin[:, 0:CH], ACT.Identity,
                                             bias=lin_bias[:, :]).then_inc(s_h0, 1)
                        keep_state(c, c)
                        stage_rows(it, k, c, 0)

                iterations(act, CITER, linear_step, peel=True)

                for layer in range(LAYERS):
                    def hand_indices(it):
                        for k in range(SLOTS):
                            n = it * SLOTS + k
                            wait_past(act, s_got[k], (it + layer * GITER) * (16 * TG))
                            nc.scalar.copy(idx[:, k, :], srcT[:, bass.ds(n * TG, TG)]).then_inc(s_idx, 1)

                    iterations(act, GITER, hand_indices, peel=layer == 0)

                    def step(it, k, first):
                        c = it * SLOTS + k
                        v = c + layer * CHUNKS
                        act.wait_ge(s_rz, v + 1)
                        act.wait_ge(s_h0, v + CHUNKS)
                        nc.scalar.activation(gr[:, :], ps_r[:, 0:CH], ACT.Sigmoid, bias=brz[:, 0:1])
                        nc.scalar.activation(gz[:, :], ps_z[:, 0:CH], ACT.Sigmoid, bias=brz[:, 1:2]).then_inc(s_rzread, 1)
                        if not first and layer < LAYERS - 1:
                            keep_state(c - 1, v + (CHUNKS - 1))
                            stage_rows(it - (k == 0), (k - 1) % SLOTS, v + (CHUNKS - 1), layer + 1)
                        act.wait_ge(s_nread, v + 1)
                        nc.scalar.activation(cand[:, :], npre[:, :], ACT.Tanh, bias=bih[:, 2:3]).then_inc(s_cand, 1)

                    for k in range(SLOTS):
                        step(0, k, k == 0)
                    with act.Fori(1, CITER) as it:
                        for k in range(SLOTS):
                            step(it, k, False)
                    if layer < LAYERS - 1:
                        keep_state(CHUNKS - 1, (layer + 2) * CHUNKS - 1)
                        stage_rows(CITER - 1, SLOTS - 1, (layer + 2) * CHUNKS - 1, layer + 1)

            @block.vector
            def _(dve):
                done = [0]

                def then(ins):
                    done[0] += 1
                    ins.then_inc(s_dve, 1)
                    dve.wait_ge(s_dve, done[0])

                dve.sem_inc(s_taken, SLOTS)
                dve.sem_inc(s_xused, SLOTS)
                dve.wait_ge(s_dst, 16)
                nc.vector.tensor_copy(dst_f, dst_rows).then_inc(s_dstf, 1)
                dve.wait_ge(s_dstf, 1)
                grouped = dst_f.rearrange("q (g n) -> q g n", n=TG * P)
                nc.vector.tensor_reduce(lo[:, :], grouped, AX.X, ALU.min)
                then(nc.vector.tensor_reduce(hi[:, :], grouped, AX.X, ALU.max))
                nc.vector.tensor_copy(lo_i[:, :], lo[:, :]).then_inc(s_lo, 1)
                nc.vector.tensor_tensor(rel_f.rearrange("q (g n) -> q g n", n=TG * P), grouped,
                                        lo[:, :].unsqueeze(2).broadcast_to([QR, TQ // TG, TG * P]),
                                        ALU.subtract).then_inc(s_rel, 1)
                then(nc.vector.tensor_tensor(hi[:, :], hi[:, :], lo[:, :], ALU.subtract))
                nc.vector.tensor_reduce(span[:, :], hi[:, :], AX.X, ALU.max).then_inc(s_span, 1)
                dve.wait_ge(s_src, 16)
                nc.vector.tensor_copy(src_rows.bitcast(fp32), src_rows).then_inc(s_srcf, 1)
                dve.wait_ge(s_spanT, 1)
                then(nc.vector.tensor_reduce(widest[:, :], ps_misc[0:1, 0:QR], AX.X, ALU.max))
                nc.vector.tensor_scalar(wide_i[:, :], widest[:, :], float(WIN), None, ALU.is_ge).then_inc(s_wide, 1)
                dve.wait_ge(s_w, 16 * 7)
                nc.vector.tensor_tensor(brz[:, :], bih[:, 0:2], bhh[:, 0:2], ALU.add).then_inc(s_dve, 1)

                def norm_step(it):
                    for k in range(SLOTS):
                        c = it * SLOTS + k
                        dve.wait_ge(s_xload[k], (it + 1) * 16)
                        wait_past(dve, s_xn, c)
                        for j in range(CJ):
                            t = nc.vector.bn_stats(stats[:, j, :], xrow[:, k, j * P:(j + 1) * P])
                        t.then_inc(s_stats, 1)
                        dve.wait_ge(s_stats, c * 2 + 1)
                        dve.sem_inc(s_passed, 1)
                        for j in range(CJ):
                            t = nc.vector.bn_aggr(mv[:, j, :], stats[:, j, :])
                        t.then_inc(s_var, 1)
                        dve.wait_ge(s_var, c + 1)
                        dve.wait_ge(s_std, c + 1)
                        nc.vector.reciprocal(rstd[:, :], rstd[:, :]).then_inc(s_stats, 1)
                        dve.wait_ge(s_stats, c * 2 + 2)
                        wait_past(dve, s_lnT, c)
                        for j in range(CJ):
                            t = nc.vector.tensor_scalar(xn[:, j * P:(j + 1) * P], xrow[:, k, j * P:(j + 1) * P],
                                                        mv[:, j, 0:1], rstd[:, j:j + 1], ALU.subtract, ALU.mult)
                        t.then_inc(s_xn, 1)
                        dve.wait_ge(s_xn, c + 1)
                        dve.sem_inc(s_xused, 1)

                iterations(dve, CITER, norm_step, peel=True)

                dve.wait_ge(s_const, 2)
                dve.wait_ge(s_eC, 3 * TQ)
                dve.wait_ge(s_bases, 16)
                wide = dve.value_load(wide_i[0:1, 0:1], min_val=0, max_val=1)

                for layer in range(LAYERS):
                    nc.vector.memset(aggT[:, :], 0.0).then_inc(s_zero, 1)
                    dve.wait_ge(s_zero, layer + 1)
                    with dve.If(wide):
                        with dve.Fori(0, GROUPS) as g:
                            nc.vector.tensor_copy(shifted[:, :], dstT[:, bass.ds(g * TG, TG)]).then_inc(s_sh, 1)
                            with dve.Fori(0, SWINS) as w:
                                m = (g + layer * GROUPS) * SWINS + w
                                dve.wait_ge(s_sh, m + (g + layer * GROUPS) + 1)
                                nc.vector.tensor_tensor(
                                    onehot_slow, iota_f[:, :].unsqueeze(1).broadcast_to([P, TG, SWIN]),
                                    shifted[:, :].unsqueeze(2).broadcast_to([P, TG, SWIN]),
                                    ALU.is_equal).then_inc(s_slow_oh, 1)
                                dve.wait_ge(s_slow_oh, m + 1)
                                nc.vector.tensor_scalar(shifted[:, :], shifted[:, :], float(SWIN), None,
                                                        ALU.subtract).then_inc(s_sh, 1)
                                dve.wait_ge(s_slow_sum, m + 1)
                                at = aggT[:, bass.ds(w * SWIN, SWIN)]
                                nc.vector.tensor_tensor(at, at, bank[0][:, 0:SWIN], ALU.add).then_inc(s_slow_add, 1)
                                dve.wait_ge(s_slow_add, m + 1)
                            dve.wait_ge(s_sh, (g + (layer * GROUPS + 1)) * (SWINS + 1))
                        dve.wait_ge(s_slow_add, (layer + 1) * GROUPS * SWINS)
                    with dve.Else():
                        with dve.Fori(0, GITER) as it:
                            for k in range(SLOTS):
                                g = it * SLOTS + k
                                n = g + layer * GROUPS
                                dve.wait_ge(s_sum, n + 1)
                                nc.vector.tensor_tensor(
                                    onehot[:, k, :].rearrange("p (t n) -> p t n", t=TG),
                                    iota_f[:, 0:WIN].unsqueeze(1).broadcast_to([P, TG, WIN]),
                                    relT[:, bass.ds(g * TG, TG)].unsqueeze(2).broadcast_to([P, TG, WIN]),
                                    ALU.is_equal).then_inc(s_oh, 1)
                                base = dve.value_load(bases[0:1, bass.ds(g, 1)], min_val=0, max_val=NODES - 1)
                                dve.wait_ge(s_sum, n + (SLOTS + 1))
                                dve.wait_ge(s_taken, n + SLOTS)
                                at = aggT[:, bass.ds(base, WIN)]
                                nc.vector.tensor_tensor(at, at, bank[k][:, 0:WIN], ALU.add).then_inc(s_taken, 1)
                        dve.wait_ge(s_taken, (layer + 1) * GROUPS + SLOTS)
                    dve.sem_inc(s_agg, 1)

                    def add_rows(it, k, c, u):
                        dve.wait_ge(s_rT, u + 1)
                        dve.wait_ge(s_xload[k], (it + (CITER + 1)) * 16)
                        dve.wait_ge(s_rS[k], (it + LAYERS * CITER) * 16)
                        nc.vector.tensor_tensor(hrow[:, k, :], ps_rows[0:CP, :], xrow[:, k, :],
                                                ALU.add).then_inc(s_rC, 1)
                        dve.wait_ge(s_rC, u + 1)
                        dve.sem_inc(s_xused, 1)

                    def step(it, k, first):
                        c = it * SLOTS + k
                        v = c + layer * CHUNKS
                        h = stateT[:, bass.ds(c * CH, CH)]
                        dve.wait_ge(s_n, v + 1)
                        dve.wait_ge(s_rzread, v + 1)
                        wait_past(dve, s_cand, v)
                        nc.vector.scalar_tensor_tensor(out=npre[:, :], in0=ps_hn[:, 0:CH], scalar=bhh[:, 2:3],
                                                       in1=gr[:, :], op0=ALU.add, op1=ALU.mult).then_inc(s_t1, 1)
                        dve.wait_ge(s_t1, v + 1)
                        nc.vector.tensor_tensor(npre[:, :], npre[:, :], ps_in[:, 0:CH], ALU.add).then_inc(s_nread, 1)
                        if not first and layer == LAYERS - 1:
                            add_rows(it - (k == 0), (k - 1) % SLOTS, c - 1, v + (CHUNKS - 1))
                        dve.wait_ge(s_cand, v + 1)
                        nc.vector.tensor_tensor(diff[:, :], h, cand[:, :], ALU.subtract).then_inc(s_d, 1)
                        dve.wait_ge(s_d, v * 2 + 1)
                        nc.vector.tensor_tensor(diff[:, :], diff[:, :], gz[:, :], ALU.mult).then_inc(s_d, 1)
                        dve.wait_ge(s_d, v * 2 + 2)
                        dve.wait_ge(s_rT, v + CHUNKS)
                        if layer < LAYERS - 1:
                            dve.wait_ge(s_keep, v + CHUNKS)
                        nc.vector.tensor_tensor(hnew[:, :], diff[:, :], cand[:, :], ALU.add).then_inc(s_h0, 1)
                        dve.wait_ge(s_h0, v + (CHUNKS + 1))

                    for k in range(SLOTS):
                        step(0, k, k == 0)
                    with dve.Fori(1, CITER) as it:
                        for k in range(SLOTS):
                            step(it, k, False)
                    if layer == LAYERS - 1:
                        add_rows(CITER - 1, SLOTS - 1, CHUNKS - 1, (layer + 2) * CHUNKS - 1)


def kernel(x, src, dst, L0_gnn_lin_w, L0_gnn_lin_b, L0_gnn_weight, L0_gnn_w_ih, L0_gnn_w_hh, L0_gnn_b_ih, L0_gnn_b_hh):
    import numpy as np
    import concourse.bacc as bacc
    from concourse import mybir as mb
    from concourse.bass_utils import run_bass_kernel_spmd

    arrays = {
        "x": np.asarray(x), "src": np.asarray(src), "dst": np.asarray(dst),
        "lin_wT": np.asarray(L0_gnn_lin_w).T, "lin_b": np.asarray(L0_gnn_lin_b),
        "weightT": np.asarray(L0_gnn_weight).transpose(0, 2, 1), "w_ihT": np.asarray(L0_gnn_w_ih).T,
        "w_hhT": np.asarray(L0_gnn_w_hh).T, "b_ih": np.asarray(L0_gnn_b_ih), "b_hh": np.asarray(L0_gnn_b_hh),
    }
    arrays = {f"in_{k}": np.ascontiguousarray(v) for k, v in arrays.items()}
    nc = bacc.Bacc("TRN2", target_bir_lowering=False, num_devices=1)
    args = [nc.dram_tensor(k, v.shape, mb.dt.from_np(v.dtype), kind="ExternalInput").ap() for k, v in arrays.items()]
    shape = arrays["in_x"].shape
    out = nc.dram_tensor("out", shape, mb.dt.float32, kind="ExternalOutput").ap()
    build(nc, *args, out, NODES=shape[0], EDGES=arrays["in_src"].shape[0], LAYERS=arrays["in_weightT"].shape[0])
    r = run_bass_kernel_spmd(nc, [arrays], core_ids=[0])
    return r.results[0]["out"]
```

```python
import concourse.bass as bass
from concourse import mybir
from contextlib import ExitStack


def build(nc, x, src, dst, lin_wT, lin_b, weightT, w_ihT, w_hhT, b_ih, b_hh, out, NODES, EDGES, LAYERS):
    fp32 = mybir.dt.float32
    bf16 = mybir.dt.bfloat16
    fp16 = mybir.dt.float16
    i32 = mybir.dt.int32
    i16 = mybir.dt.int16
    ALU = mybir.AluOpType
    ACT = mybir.ActivationFunctionType
    AX = mybir.AxisListType

    P = 128
    PARTS = 3
    TILES = EDGES // P
    TG = 5
    GROUPS = TILES // TG
    SLOTS = 5
    GITER = GROUPS // SLOTS
    QR = 125
    TQ = TILES // QR
    GQ = TQ // TG
    WIN = 128
    SWIN = 512
    SWINS = -(-NODES // SWIN)
    CH = 500
    CP = 125
    CJ = CH // CP
    CHUNKS = NODES // CH
    CITER = CHUNKS // SLOTS
    BLOCKS = -(-NODES // P)
    SUB = 4
    SW = SUB * BLOCKS
    UT = 2
    DWINS = 60
    PER = P // SUB
    UNITS = DWINS * PER
    UC = UNITS // P
    STRIPS = UNITS
    SPL = 4
    BODY = 4
    ITERS = 3
    DLOOPS = DWINS // BODY
    DITER = DLOOPS * ITERS
    BPS = BODY * BLOCKS / (ITERS * SLOTS)
    LATER = 16
    OB = 4
    PAIRS = PER // 2
    ON_VECTOR = 4
    PIECES = 7
    BIG = 4096
    AHEAD = 3
    AGGW = max(SWINS * SWIN, NODES + WIN, 4 * TQ * P)
    EPS = 1e-5
    THR_STEP = 160
    assert 2 * STRIPS < BIG and STRIPS * SUB + P <= NODES and UNITS % P == 0 and PAIRS % OB == 0 and DWINS % 2 == 0
    assert UT == 2 and UNITS * BIG < 2 ** 24 and DLOOPS * BODY == DWINS
    assert TILES * P == EDGES and GITER * SLOTS * TG == TILES and TQ * QR == TILES
    assert CITER * SLOTS * CH == NODES and TQ % TG == 0 and STRIPS % THR_STEP == 0

    ctx = ExitStack()
    with ctx:
        def sb(name, shape, dt=fp32):
            return ctx.enter_context(nc.sbuf_tensor(name, shape, dt))

        def sem(name):
            return ctx.enter_context(nc.semaphore(name))

        def sems(name, n=SLOTS):
            return [sem(f"{name}{k}") for k in range(n)]

        def dram(name, shape, dt):
            return nc.dram_tensor(name, shape, dt, kind="Internal").ap()

        table = dram("table", [BLOCKS * P, PARTS * P], bf16)
        state = dram("state", [P, NODES], fp32)
        counts = dram("counts", [DWINS, P, BLOCKS * P], bf16)
        bases_dram = dram("bases_dram", [QR, GQ], i32)
        lows_dram = dram("lows_dram", [QR, GQ], fp32)
        mins_dram = dram("mins_dram", [QR + 1, TQ], fp32)
        edge_rows = dram("edge_rows", [TILES + 1, 2 * P], fp32)

        aggT = sb("aggT", [P, AGGW])
        srcT = sb("srcT", [P, TILES], i16)
        dstT = sb("dstT", [P, TILES], i16)
        relT = sb("relT", [P, TILES], bf16)
        idx = sb("idx", [P, SLOTS, TG], i32)
        iota_b = sb("iota_b", [P, WIN], bf16)
        iota_s = sb("iota_s", [P, SWIN])
        shifted = sb("shifted", [P, TG])
        ident = sb("ident", [P, P])
        ones = sb("ones", [P, P])
        bases = sb("bases", [1, GROUPS], i32)
        wide_i = sb("wide_i", [1, 1], i32)
        skip_i = sb("skip_i", [1, 4], i32)
        verdict = sb("verdict", [P, 8])
        ok_b, limit_b, reached, spared = (verdict[:, i:i + 1] for i in range(4))
        digit = verdict[:, 4:5]
        ulist = sb("ulist", [P, 5, UC])
        unit_no, unit_sum, unit_strip, unit_tile, unit_live = (ulist[:, i, :] for i in range(5))
        ulist_i = sb("ulist_i", [P, UC], i32)
        unit_idx = sb("unit_idx", [P, UC, UT], i32)
        unit_shift = sb("unit_shift", [P, UC, UT])
        relcol = sb("relcol", [P, DWINS])
        dbases = sb("dbases", [1, DWINS], i32)
        select = sb("select", [P, P])
        whh_sb = sb("whh_sb", [P, 3 * P])
        comb = sb("comb", [P, LAYERS, 3 * P])
        lin_sb = sb("lin_sb", [P, P])
        lin_bias = sb("lin_bias", [P, 1])
        bih = sb("bih", [P, 3])
        bhh = sb("bhh", [P, 3])
        brz = sb("brz", [P, 2])
        eps_t = sb("eps_t", [P, 1])
        stats = sb("stats", [CP, CJ, 6])
        mv = sb("mv", [CP, CJ, 2])
        rstd = sb("rstd", [CP, CJ])
        dsum = sb("dsum", [P, P])
        tmin = sb("tmin", [QR, TQ])
        tmax = sb("tmax", [QR, TQ])
        big = sb("big", [1, TQ])
        lo = sb("lo", [QR, GQ])
        hi = sb("hi", [QR, GQ])
        lo_i = sb("lo_i", [QR, GQ], i32)
        checks = sb("checks", [QR, 2])

        def carve(tensor, wanted):
            at, found = 0, {}
            for name, (n, dt) in wanted.items():
                k = n * (2 if dt in (fp32, i32) else 1)
                v = tensor[:, at:at + k]
                found[name] = v if dt == bf16 else v.bitcast(dt)
                at += k
            assert at <= tensor.shape[1], (at, tensor.shape)
            return found

        rows_s = sb("rows_s", [P, SLOTS * TG * PARTS * P], bf16)
        rows = rows_s[:, :].rearrange("p (s t n) -> p s t n", s=SLOTS, t=TG)
        gates_v = carve(rows_s, {f"g{i}": (CH, fp32) for i in range(5)})
        gr, gz, npre, cand, diff = (gates_v[f"g{i}"] for i in range(5))
        slo_f = carve(rows_s, {"v": (TQ * P, fp32)})["v"][0:QR, :]
        onehot_s = sb("onehot_s", [P, SLOTS * TG * P], bf16)
        onehot = onehot_s[:, :].rearrange("p (s n) -> p s n", s=SLOTS)
        onehot_slow = onehot_s[:, 0:TG * SWIN].rearrange("p (t n) -> p t n", n=SWIN)
        start_v = carve(onehot_s, {"pattern": (SWIN, i32), "zpad": (PARTS * P, bf16), "padrow": (2 * P, fp32),
                                   "tnext": (TQ, fp32)})
        pattern, zpad = start_v["pattern"], start_v["zpad"][0:BLOCKS * P - NODES, :]
        padrow, tnext = start_v["padrow"][0:1, :], start_v["tnext"][0:QR, :]
        win_s = sb("win_s", [P, P * BLOCKS], bf16)
        window = win_s[:, :].rearrange("p (b d) -> p b d", b=BLOCKS)
        win_bufs = [win_s[:, :], aggT[:, 0:P * BLOCKS // 2].bitcast(bf16)]
        reach = [aggT[:, 0:STRIPS], aggT[:, STRIPS:2 * STRIPS]]
        gathered = aggT[:, 2 * STRIPS:2 * STRIPS + UC * UT * 2 * P]
        win_v = carve(win_s, {"hs": (SLOTS * CH, fp32), "xn": (CJ * P, fp32), "lnT": (CH, fp32),
                              "rest": (CJ * P, fp32)})
        hs = win_v["hs"].rearrange("p (s n) -> p s n", s=SLOTS)
        xn, lnT, rest = win_v["xn"][0:CP, :], win_v["lnT"], win_v["rest"][0:CP, :]
        keys_v = carve(win_s, {"key": (TQ * P, fp32), "below": (THR_STEP * TQ, bf16)})
        key_f, below = keys_v["key"][0:QR, :], keys_v["below"][0:QR, :]
        parts_s = sb("parts_s", [P, BLOCKS * PARTS * P], bf16)
        parts = parts_s[:, :].rearrange("p (b n) -> p b n", b=BLOCKS)
        wv = carve(parts_s, {"key": (UNITS * UT, fp32), "slo": (UNITS * UT, bf16), "lo_b": (GROUPS, fp32),
                             "iota_w": (SW, fp16), "kw": (PER * UT, fp32), "sw": (2 * PER * UT, fp32), "setup": ((LAYERS + 3) * P, fp32),
                             "xrow": (SLOTS * CJ * P, fp32), "ol": (2 * 4 * UT * P, bf16),
                             "hrow": (SLOTS * CJ * PARTS * P, bf16), "oh": (OB * 2 * UT * SW, bf16)})
        keyT, sloT, lo_b, iota_w, kw, ol, oh = (wv[n] for n in ("key", "slo", "lo_b", "iota_w", "kw", "ol", "oh"))
        ohv = oh.rearrange("p (o t n) -> p o t n", o=OB, t=2 * UT)
        olv = ol.rearrange("p (o t n) -> p o t n", o=2, t=4 * UT)
        sw = wv["sw"].rearrange("p (o n) -> p o n", o=2)
        key_units = keyT.rearrange("p (q i) -> p i q", i=UT)
        slo_units = sloT.rearrange("p (q i) -> p i q", i=UT)
        before = 2 * (UNITS * UT + GROUPS + 3 * PER * UT + (LAYERS + 3) * P + SLOTS * CJ * P) + UNITS * UT + SW + 8 * UT * P
        found_v = carve(parts_s[:, before:], {"cnt": (STRIPS, fp32), "delta": (STRIPS, fp32), "code": (STRIPS, fp32),
                                              "scratch": (STRIPS, fp32)})
        cnt, delta, code, scratch = found_v["cnt"][0:QR, :], found_v["delta"], found_v["code"], found_v["scratch"]
        pattern_s = delta.bitcast(i32)
        xrow = wv["xrow"][0:CP, :].rearrange("p (s n) -> p s n", s=SLOTS)
        hrow = wv["hrow"][0:CP, :].rearrange("p (s n) -> p s n", s=SLOTS)
        hrow_f = wv["hrow"][0:CP, :].bitcast(fp32).rearrange("p (s n) -> p s n", s=SLOTS)
        set_v = carve(wv["setup"].bitcast(bf16), {"wT": (LAYERS * P, fp32), "wih": (3 * P, fp32)})
        wT_sb, wih_sb = set_v["wT"].rearrange("p (l n) -> p l n", l=LAYERS), set_v["wih"]
        EW = TQ * P
        src_rows = aggT[0:QR, 0:EW].bitcast(i32)
        dst_rows = aggT[0:QR, EW:2 * EW].bitcast(i32)
        src_f = aggT[0:QR, EW:2 * EW]
        dst_f = aggT[0:QR, 2 * EW:3 * EW]
        rel_f = aggT[0:QR, 3 * EW:4 * EW]
        by_g = lambda a: a.rearrange("p (q g) -> p g q", g=TQ)
        u_slot = [0]

        def part_of(k, part):
            return hrow[:, k, :].rearrange("p (j n) -> p j n", j=CJ)[:, :, part * P:(part + 1) * P]

        sums = [ctx.enter_context(nc.psum_tensor(f"sums{i}", [P, 512], fp32)) for i in range(3)]
        pair = [ctx.enter_context(nc.psum_tensor(f"pair{i}", [P, 1024], fp32)) for i in range(2)]
        ps_misc = ctx.enter_context(nc.psum_tensor("ps_misc", [P, 512], fp32))
        ps_r, ps_z, ps_in = sums
        ps_hn, ps_rows = pair[0][:, 0:512], pair[0][:, 512:1024]
        ps_ln, ps_lin = pair[1][:, 0:512], pair[1][:, 512:1024]
        ps_dense = [pair[1][:, i * 512:i * 512 + PARTS * P] for i in range(2)]
        ps_denseT = pair[0][:, 512:512 + P]
        banks4 = [pair[0][:, 0:512], pair[0][:, 512:1024], pair[1][:, 0:512], pair[1][:, 512:1024]]
        BANK = [0, 1, 2, 0, 1]

        s_src, s_dst, s_w = sem("src_loaded"), sem("dst_loaded"), sem("weights_loaded")
        s_const, s_iota = sem("constants_ready"), sem("iota_written")
        s_dve = sem("dve_setup_step")
        s_dstf, s_srcf, s_rel = sem("dst_as_float"), sem("src_as_float"), sem("rel_ready")
        s_slo, s_key = sem("slo_ready"), sem("key_ready")
        s_lo, s_lo_st, s_bases = sem("bases_int_ready"), sem("bases_stored"), sem("bases_loaded")
        s_min, s_min_st, s_next = sem("mins_ready"), sem("mins_stored"), sem("next_mins_loaded")
        s_cnt, s_cntP, s_strips = sem("below_counted"), sem("below_summed"), sem("strip_starts_ready")
        s_chk, s_chkP, s_wide = sem("checks_ready"), sem("checks_summed"), sem("wide_flag_ready")
        s_rows, s_uidx, s_ugot = sem("edge_rows_stored"), sem("unit_indices_ready"), sem("unit_tiles_gathered")
        s_ushift, s_uT, s_uC = sem("unit_keys_shifted"), sem("unit_lists_transposed"), sem("unit_lists_copied")
        s_relm, s_relP, s_relC = sem("placing_ready"), sem("columns_placed"), sem("columns_ready")
        s_kw, s_sw = sem("window_keys_ready"), sem("window_digits_ready")
        s_eT, s_eC = sem("edges_transposed"), sem("edges_copied")
        s_comb, s_combC = sem("combined_product"), sem("combined_copied")
        s_xload = sems("x_loaded")
        s_xused = sem("x_used")
        s_stats, s_var, s_std, s_xn = sem("ln_step"), sem("variance_ready"), sem("std_ready"), sem("x_normed")
        s_lnT, s_lnC, s_lin = sem("ln_transposed"), sem("ln_copied"), sem("linear_product")
        s_h0 = sem("state_written")
        s_kS = sems("state_stored")
        s_hload = sems("state_loaded")
        s_rT, s_hi, s_rest, s_mid, s_rC = (sem("rows_transposed"), sem("rows_hi"), sem("rows_rest"), sem("rows_mid"),
                                           sem("rows_staged"))
        s_rS = sems("rows_stored")
        s_pad = sem("table_padded")
        s_idx = sem("indices_ready")
        s_got = sems("rows_gathered")
        s_sum, s_taken, s_oh = sem("group_summed"), sem("sums_taken"), sem("onehot_ready")
        s_zero, s_agg = sem("agg_zeroed"), sem("layer_aggregated")
        s_sh, s_slow_oh = sem("slow_shifted"), sem("slow_onehot_ready")
        s_slow_sum, s_slow_add = sem("slow_window_summed"), sem("slow_window_added")
        s_boh, s_bol, s_bsum, s_evac = (sem("unit_dst_onehot_ready"), sem("unit_src_onehot_ready"), sem("unit_pair_counted"),
                                        sem("unit_pair_copied"))
        s_aS, s_winfree = sem("window_stored"), sem("window_free")
        s_steer, s_lob = sem("steering_ready"), sem("lows_loaded")
        s_parts = sems("parts_loaded", PIECES)
        s_aL, s_used = sems("window_loaded", PIECES), sems("window_used", PIECES)
        s_dpart, s_dcopy, s_sel, s_dT, s_dadd = sem("dense_part_added"), sem("dense_copied"), sem("selection_ready"), sem("dense_transposed"), sem("dense_added")
        s_rz, s_n = sem("rz_product"), sem("n_product")
        s_rzread, s_nread = sem("gates_ready"), sem("n_pre_ready")
        s_t1, s_cand, s_d = sem("reset_applied"), sem("candidate_ready"), sem("update_step")
        s_passed = sem("wait_passed")

        def chunk_rows(t, c):
            return t[0:NODES, :].rearrange("(c p j) f -> p c (j f)", p=CP, j=CJ)[:, bass.ds(c, 1), :].rearrange(
                "p o n -> p (o n)")

        def wait_past(eng, semaphore, value):
            if isinstance(value, int) and value == 0:
                return
            eng.wait_ge(semaphore, value)

        def iterations(eng, count, body, peel):
            if peel:
                body(0)
            with eng.Fori(1 if peel else 0, count) as it:
                body(it)

        def steps(eng, count, step):
            for k in range(SLOTS):
                step(0, k, k == 0)
            with eng.Fori(1, count) as it:
                for k in range(SLOTS):
                    step(it, k, False)

        def load_skip(eng):
            eng.wait_ge(s_steer, 1)
            return (eng.value_load(skip_i[0:1, 0:1], min_val=0, max_val=GITER - DITER - 1),
                    eng.value_load(skip_i[0:1, 1:2], min_val=DITER + 1, max_val=GITER))

        def load_last(eng):
            return (eng.value_load(skip_i[0:1, 2:3], min_val=DITER, max_val=GITER - 1),
                    eng.value_load(skip_i[0:1, 3:4], min_val=0, max_val=GITER - DITER - 1))

        def iteration(skip, i):
            return nc.s_assert_within(skip + i, 0, GITER - 1,
                                      skip_runtime_bounds_check_because="i is below kept, and skip + kept is GITER")

        def block_range(s):
            return [divmod(g, BLOCKS) for g in range(int(BPS * s + 0.001), int(BPS * (s + 1) + 0.001))]

        def ends_in(s):
            return [("sum", a) if b == BLOCKS - 1 else ("add", a - 1) for a, b in block_range(s) if b in (BLOCKS - 1, LATER)]

        def piece(b):
            return b * PIECES // BLOCKS

        with nc.Block() as block:

            @block.sync
            def _(sp):
                sp.dma_start(dst_rows, dst.rearrange("(q n) -> q n", q=QR)).then_inc(s_dst, 16)
                sp.dma_start(src_rows, src.rearrange("(q n) -> q n", q=QR)).then_inc(s_src, 16)
                sp.dma_start(wT_sb, weightT.rearrange("l k f -> k l f")).then_inc(s_w, 16)
                sp.dma_start(wih_sb, w_ihT).then_inc(s_w, 16)
                sp.dma_start(whh_sb[:, :], w_hhT).then_inc(s_w, 16)
                sp.dma_start(lin_sb[:, :], lin_wT).then_inc(s_w, 16)
                with nc.allow_non_contiguous_dma(reason="biases, one per partition"):
                    sp.dma_start(lin_bias[:, :], lin_b.rearrange("(p o) -> p o", o=1)).then_inc(s_w, 16)
                    sp.dma_start(bih[:, :], b_ih.rearrange("(g p) -> p g", p=P)).then_inc(s_w, 16)
                    sp.dma_start(bhh[:, :], b_hh.rearrange("(g p) -> p g", p=P)).then_inc(s_w, 16)
                sp.wait_ge(s_const, 8)
                sp.dma_start(table[NODES:BLOCKS * P, :], zpad).then_inc(s_pad, 16)
                sp.dma_start(edge_rows[TILES:TILES + 1, :], padrow).then_inc(s_rows, 16)
                sp.wait_ge(s_min, 1)
                sp.dma_start(mins_dram[0:QR, :], tmin[:, :]).then_inc(s_min_st, 16)
                sp.dma_start(mins_dram[QR:QR + 1, :], big[:, :]).then_inc(s_min_st, 16)
                sp.wait_ge(s_min_st, 32)
                sp.dma_start(tnext, mins_dram.rearrange("a b -> (a b)")[1:TILES + 1].rearrange(
                    "(q g) -> q g", g=TQ)).then_inc(s_next, 16)
                sp.wait_ge(s_lo, 1)
                sp.dma_start(bases_dram, lo_i[:, :]).then_inc(s_lo_st, 16)
                sp.dma_start(lows_dram, lo[:, :]).then_inc(s_lo_st, 16)
                sp.wait_ge(s_lo_st, 32)
                sp.dma_start(bases[:, :], bases_dram.rearrange("(o q) g -> o (q g)", o=1)).then_inc(s_bases, 16)
                sp.dma_start(lo_b, lows_dram.rearrange("(o q) g -> o (q g)", o=1).to_broadcast([P, GROUPS])).then_inc(s_lob, 16)
                by_tile = edge_rows[0:TILES, :].rearrange("(q g) n -> q g n", g=TQ)
                for i, (what, ready) in enumerate(((key_f, s_key), (slo_f, s_slo))):
                    sp.wait_ge(ready, 1)
                    sp.dma_start(by_tile[:, :, i * P:(i + 1) * P], what.rearrange("q (g n) -> q g n", n=P)).then_inc(s_rows, 16)

                def store_chunks(stage):
                    with sp.Fori(0, CITER) as it:
                        for k in range(SLOTS):
                            c = it * SLOTS + k
                            if stage < LAYERS:
                                sp.wait_ge(s_h0, c + (stage * CHUNKS + 1))
                                sp.dma_start(state[:, bass.ds(c * CH, CH)], hs[:, k, :]).then_inc(s_kS[k], 16)
                            sp.wait_ge(s_rC, c + (stage * CHUNKS + 1))
                            if stage < LAYERS:
                                sp.dma_start(chunk_rows(table, c), hrow[:, k, :]).then_inc(s_rS[k], 16)
                            else:
                                sp.dma_start(chunk_rows(out, c), hrow_f[:, k, 0:CJ * P]).then_inc(s_rS[k], 16)

                store_chunks(0)
                sp.wait_ge(s_wide, 1)
                wide = sp.value_load(wide_i[0:1, 0:1], min_val=0, max_val=1)
                sp.wait_ge(s_pad, 16)
                with sp.Fori(0, DWINS // 2) as i:
                    for o in range(2):
                        w = i * 2 + o
                        sp.wait_ge(s_evac, w * PAIRS + (PAIRS + 2))
                        sp.dma_start(counts[bass.ds(w, 1), :, :].rearrange("w p n -> p (w n)"),
                                     win_bufs[o]).then_inc(s_aS, 16)
                        sp.wait_ge(s_aS, w * 16 + 16)
                        sp.sem_inc(s_winfree, 1)

                def load_window(layer, j, with_parts=False):
                    w = j + layer * DWINS
                    for h in range(PIECES):
                        b = [b for b in range(BLOCKS) if piece(b) == h]
                        n = slice(b[0] * P, (b[-1] + 1) * P)
                        if with_parts:
                            sp.dma_start(parts[:, b[0]:b[-1] + 1, :],
                                         table.rearrange("(b p) n -> p b n", p=P)[:, b[0]:b[-1] + 1, :]).then_inc(
                                s_parts[h], 16)
                        wait_past(sp, s_used[h], w)
                        sp.dma_start(win_s[:, n], counts[bass.ds(j, 1), :, n].rearrange("w p n -> p (w n)")).then_inc(
                            s_aL[h], 16)

                for stage in range(1, LAYERS + 1):
                    for k in range(SLOTS):
                        sp.wait_ge(s_rS[k], 16 * CITER * stage)
                        sp.wait_ge(s_kS[k], 16 * CITER * stage)
                    with sp.If(wide):
                        sp.sem_inc(s_passed, 1)
                    with sp.Else():
                        sp.wait_ge(s_aS, 16 * DWINS)
                        load_window(stage - 1, 0, with_parts=True)
                        with sp.Fori(1, DWINS) as j:
                            load_window(stage - 1, j)
                    store_chunks(stage)
                for k in range(SLOTS):
                    sp.wait_ge(s_rS[k], 16 * CITER * (LAYERS + 1))
                    sp.wait_ge(s_kS[k], 16 * CITER * LAYERS)

            @block.gpsimd
            def _(pool):
                nc.gpsimd.memset(ident[:, :], 0.0).then_inc(s_iota, 1)
                nc.gpsimd.iota(pattern, pattern=[[1, SWIN]], base=0, channel_multiplier=0).then_inc(s_iota, 1)
                nc.gpsimd.memset(eps_t[:, :], EPS).then_inc(s_const, 1)
                nc.gpsimd.memset(ones[:, :], 1.0).then_inc(s_const, 1)
                nc.gpsimd.memset(zpad, 0.0).then_inc(s_const, 1)
                nc.gpsimd.memset(padrow, -1.0).then_inc(s_const, 1)
                nc.gpsimd.memset(big[:, :], 1.0e9).then_inc(s_const, 1)
                pool.wait_ge(s_iota, 2)
                nc.gpsimd.tensor_copy(iota_w, pattern[:, 0:SW]).then_inc(s_iota, 1)
                nc.gpsimd.tensor_copy(iota_b[:, :], pattern[:, 0:WIN]).then_inc(s_iota, 1)
                nc.gpsimd.tensor_copy(iota_s[:, :], pattern[:, 0:SWIN]).then_inc(s_iota, 1)
                nc.gpsimd.affine_select(out=ident[:, :], in_=ident[:, :], compare_op=ALU.not_equal, fill=1.0, base=0,
                                        pattern=[[-1, P]], channel_multiplier=1).then_inc(s_const, 1)
                pool.wait_ge(s_iota, 5)
                nc.gpsimd.iota(pattern_s, pattern=[[SUB, STRIPS]], base=SUB, channel_multiplier=0).then_inc(s_iota, 1)
                pool.wait_ge(s_iota, 6)
                nc.gpsimd.tensor_copy(scratch, pattern_s).then_inc(s_const, 1)
                nc.gpsimd.iota(ulist_i[:, :], pattern=[[P, UC]], base=0, channel_multiplier=1).then_inc(s_iota, 1)
                pool.wait_ge(s_iota, 7)
                nc.gpsimd.tensor_copy(unit_no, ulist_i[:, :]).then_inc(s_const, 1)

                def load_x(uses):
                    with pool.Fori(0, CITER) as it:
                        for k in range(SLOTS):
                            c = it * SLOTS + k
                            pool.wait_ge(s_xused, c + uses * CHUNKS + 1)
                            pool.dma_start(xrow[:, k, :], chunk_rows(x, c)).then_inc(s_xload[k], 16)
                            if uses:
                                load_state(LAYERS - 1, it, k)

                def load_state(layer, it, k):
                    c = it * SLOTS + k
                    if layer < LAYERS - 1:
                        pool.wait_ge(s_kS[k], (it + (layer + 1) * CITER) * 16)
                    else:
                        pool.wait_ge(s_kS[k], 16 * CITER * LAYERS)
                    pool.wait_ge(s_rT, c + ((layer + 1) * CHUNKS - SLOTS + 1))
                    pool.dma_start(hs[:, k, :], state[:, bass.ds(c * CH, CH)]).then_inc(s_hload[k], 16)

                pool.wait_ge(s_rows, 48)
                pool.wait_ge(s_uidx, 1)
                pool.sem_inc(s_passed, 1)
                for c in range(UC):
                    for i in range(UT):
                        at = (c * UT + i) * 2 * P
                        pool.indirect_dma_start(gathered[:, at:at + 2 * P], None, edge_rows,
                                                bass.IndirectOffsetOnAxis(ap=unit_idx[:, c, i:i + 1], axis=0)).then_inc(s_ugot, 16)
                load_x(0)
                pool.wait_ge(s_uC, 2 * UC)
                pool.sem_inc(s_passed, 1)
                with pool.Fori(0, DWINS // 2) as i:
                  for o in range(2):
                    w = i * 2 + o
                    pool.wait_ge(s_sw, w + 1)
                    pool.sem_inc(s_passed, 1)
                    for m in range(PAIRS // 2):
                        b = w * PAIRS + m * 2
                        pool.wait_ge(s_bsum, b + 2)
                        pool.sem_inc(s_passed, 1)
                        for t in range(ON_VECTOR, 4 * UT):
                            ins = nc.gpsimd.tensor_scalar(olv[:, m % 2, t, :], iota_b[:, :],
                                                          sw[:, o, m * 4 * UT + t:m * 4 * UT + t + 1], None, ALU.is_equal)
                        ins.then_inc(s_bol, 1)
                skip, kept = load_skip(pool)
                for layer in range(LAYERS):
                    for k in range(SLOTS):
                        pool.wait_ge(s_rS[k], 16 * CITER * (layer + 1))
                    with pool.Fori(0, kept) as i:
                        u = i + kept * layer if layer else i
                        for k in range(SLOTS):
                            n = u * SLOTS + k
                            pool.wait_ge(s_idx, n + 1)
                            pool.wait_ge(s_sum, n + 1)
                            pool.sem_inc(s_passed, 1)
                            for j in range(TG):
                                pool.indirect_dma_start(
                                    rows[:, k, j, :], None, table,
                                    bass.IndirectOffsetOnAxis(ap=idx[:, k, j:j + 1], axis=0)).then_inc(s_got[k], 16)
                    pool.wait_ge(s_agg, layer + 1)
                    if layer < LAYERS - 1:
                        with pool.Fori(0, CITER) as it:
                            for k in range(SLOTS):
                                load_state(layer, it, k)
                    else:
                        load_x(1)

            @block.tensor
            def _(pe):
                pe.sem_inc(s_sum, SLOTS)
                pe.sem_inc(s_bsum, OB)
                pe.wait_ge(s_const, 8)

                n = 0
                for what, ready in ((dst_f, s_dstf), (rel_f, s_rel), (src_f, s_srcf)):
                    pe.wait_ge(ready, 1)
                    for g in range(TQ):
                        if n >= 2:
                            pe.wait_ge(s_eC, n - 1)
                        nc.tensor.transpose(sums[n % 2][:, 0:QR], what[:, g * P:(g + 1) * P],
                                            ident[0:QR, 0:QR]).then_inc(s_eT, 1)
                        n += 1
                pe.wait_ge(s_chk, 1)
                nc.tensor.matmul(ps_misc[:, 0:2], ones[0:QR, :], checks[:, :], start=True, stop=True).then_inc(s_chkP, 1)
                pe.wait_ge(s_cnt, STRIPS // THR_STEP)
                for i in range(SPL):
                    w = STRIPS // SPL
                    t = nc.tensor.matmul(banks4[i][:, 0:w], ones[0:QR, :], cnt[:, i * w:(i + 1) * w],
                                         start=True, stop=True)
                t.then_inc(s_cntP, 1)

                pe.wait_ge(s_w, 16 * 7)
                pe.wait_ge(s_eC, n)
                for layer in range(LAYERS):
                    nc.tensor.matmul(sums[layer][:, 0:3 * P], wT_sb[:, layer, :], wih_sb, start=True,
                                     stop=True).then_inc(s_comb, 1)
                pe.wait_ge(s_strips, 1)
                for k in range(P // PER):
                    pe.wait_ge(s_relm, k + 1)
                    nc.tensor.matmul(ps_misc[:, k * UC:(k + 1) * UC], select[:, :], unit_strip, start=True, stop=True)
                    nc.tensor.matmul(ps_misc[0:1, (4 + k) * UC:(5 + k) * UC], ident[:, k * PER:k * PER + 1], unit_strip,
                                     start=True, stop=True).then_inc(s_relP, 1)
                pe.wait_ge(s_combC, 1)
                pe.wait_ge(s_ushift, 1)
                for c in range(UC):
                    if c >= 2:
                        pe.wait_ge(s_uC, 2 * c - 2)
                    for half in range(2):
                        for i in range(UT):
                            at = (c * UT + i) * 2 * P + half * P
                            t = nc.tensor.transpose(sums[c % 2][:, (half * UT + i) * P:(half * UT + i + 1) * P],
                                                    gathered[:, at:at + P], ident[:, :])
                    t.then_inc(s_uT, 1)

                def transpose_rows(k, u):
                    pe.wait_ge(s_h0, u + 1)
                    wait_past(pe, s_rest, u)
                    for j in range(CJ):
                        t = nc.tensor.transpose(ps_rows[0:CP, j * P:(j + 1) * P], hs[:, k, bass.ds(j, CP, CJ)],
                                                ident[:, :])
                    t.then_inc(s_rT, 1)

                def linear_step(it, k, first):
                    c = it * SLOTS + k
                    pe.wait_ge(s_xn, c + 1)
                    wait_past(pe, s_lnC, c)
                    for j in range(CJ):
                        t = nc.tensor.transpose(ps_ln[:, j * CP:(j + 1) * CP], xn[:, j * P:(j + 1) * P],
                                                ident[0:CP, 0:CP])
                    t.then_inc(s_lnT, 1)
                    if not first:
                        transpose_rows((k - 1) % SLOTS, c - 1)
                    pe.wait_ge(s_lnC, c + 1)
                    wait_past(pe, s_h0, c)
                    nc.tensor.matmul(ps_lin[:, 0:CH], lin_sb[:, :], lnT, start=True, stop=True).then_inc(s_lin, 1)

                steps(pe, CITER, linear_step)
                transpose_rows(SLOTS - 1, CHUNKS - 1)
                pe.wait_ge(s_wide, 1)
                wide = pe.value_load(wide_i[0:1, 0:1], min_val=0, max_val=1)

                def group_product(u, k):
                    n = u * SLOTS + k
                    pe.wait_ge(s_oh, n + 1)
                    pe.wait_ge(s_taken, n + 1)
                    pe.wait_ge(s_got[k], (u + 1) * (16 * TG))
                    for j in range(TG):
                        for part in range(PARTS):
                            t = nc.tensor.matmul(sums[BANK[k]][:, 0:WIN], rows[:, k, j, part * P:(part + 1) * P],
                                                 onehot[:, k, j * P:(j + 1) * P], start=(j == 0 and part == 0),
                                                 stop=(j == TG - 1 and part == PARTS - 1))
                    t.then_inc(s_sum, 1)

                def build_window(w):
                    for m in range(PAIRS):
                        b = w * PAIRS + m
                        pe.wait_ge(s_evac, b + 1)
                        pe.wait_ge(s_boh, b + 2)
                        if m % 2 == 0:
                            pe.wait_ge(s_bol, w * (PAIRS // 2) + (m // 2 + 1 + PAIRS))
                        for j in range(2):
                            for i in range(UT):
                                t = nc.tensor.matmul(pair[m % 2][:, j * 512:j * 512 + SW],
                                                     olv[:, m // 2 % 2, (m % 2 * 2 + j) * UT + i, :],
                                                     ohv[:, m % OB, j * UT + i, :], start=(i == 0), stop=(i == UT - 1))
                        t.then_inc(s_bsum, 1)

                def dense_block(w, a, b):
                    if b == 0:
                        wait_past(pe, s_dcopy, max(w - 1, 0) if isinstance(w, int) else w - 1)
                    if b == 0 or piece(b) != piece(b - 1):
                        pe.wait_ge(s_aL[piece(b)], (w + 1) * 16)
                        if isinstance(w, int):
                            pe.wait_ge(s_parts[piece(b)], (w // DWINS + 1) * 16)
                    t = nc.tensor.matmul(ps_dense[a % 2], window[:, b, :], parts[:, b, :], start=(b == 0),
                                         stop=(b == BLOCKS - 1))
                    if b == BLOCKS - 1 or piece(b) != piece(b + 1):
                        t.then_inc(s_used[piece(b)], 1)

                def dense_transpose(w):
                    pe.wait_ge(s_sel, w + 1)
                    pe.wait_ge(s_dcopy, w + 1)
                    wait_past(pe, s_dadd, w)
                    nc.tensor.matmul(ps_denseT, dsum[:, :], select[:, :], start=True, stop=True).then_inc(s_dT, 1)

                def slow_groups(layer):
                    with pe.Fori(0, GITER) as it:
                        for k in range(SLOTS):
                            n = it * SLOTS + (k + layer * GROUPS)
                            pe.wait_ge(s_got[k], (it + (layer * GITER + 1)) * (16 * TG))
                            pe.sem_inc(s_passed, 1)
                            with pe.Fori(0, SWINS) as w:
                                pe.wait_ge(s_slow_oh, n * SWINS + w + 1)
                                for j in range(TG):
                                    for part in range(PARTS):
                                        t = nc.tensor.matmul(sums[0][:, 0:SWIN], rows[:, k, j, part * P:(part + 1) * P],
                                                             onehot_slow[:, j, :], start=(j == 0 and part == 0),
                                                             stop=(j == TG - 1 and part == PARTS - 1))
                                t.then_inc(s_slow_sum, 1)
                            pe.wait_ge(s_slow_sum, (n + 1) * SWINS)
                            pe.sem_inc(s_sum, 1)

                with pe.Fori(0, DWINS) as w:
                    build_window(w)
                skip, kept = load_skip(pe)
                for layer in range(LAYERS):
                    with pe.If(wide):
                        slow_groups(layer)
                    with pe.Else():
                        past = kept * layer if layer else 0

                        def dense_step(d):
                            for s in range(ITERS * SLOTS):
                                group_product(past + d * ITERS + s // SLOTS, s % SLOTS)
                                for a, b in block_range(s):
                                    w = d * BODY + (a + layer * DWINS)
                                    dense_block(w, a, b)
                                    if b == LATER and not (isinstance(d, int) and a == 0):
                                        dense_transpose(w - 1)

                        iterations(pe, DLOOPS, dense_step, peel=True)
                        dense_transpose(layer * DWINS + (DWINS - 1))
                        with pe.Fori(DITER, kept) as i:
                            for k in range(SLOTS):
                                group_product(past + i, k)

                    pe.wait_ge(s_agg, layer + 1)

                    def gates(it, k):
                        c = it * SLOTS + k
                        v = c + layer * CHUNKS
                        h = hs[:, k, :]
                        a = aggT[:, bass.ds(c * CH, CH)]
                        pe.wait_ge(s_hload[k], (it + (layer * CITER + 1)) * 16)
                        wait_past(pe, s_rzread, v)
                        for g, ps in ((0, ps_r), (1, ps_z)):
                            nc.tensor.matmul(ps[:, 0:CH], comb[:, layer, g * P:(g + 1) * P], a, start=True, stop=False)
                            t = nc.tensor.matmul(ps[:, 0:CH], whh_sb[:, g * P:(g + 1) * P], h, start=False, stop=True)
                        t.then_inc(s_rz, 1)
                        wait_past(pe, s_nread, v)
                        nc.tensor.matmul(ps_in[:, 0:CH], comb[:, layer, 2 * P:3 * P], a, start=True, stop=True)
                        nc.tensor.matmul(ps_hn[:, 0:CH], whh_sb[:, 2 * P:3 * P], h, start=True,
                                         stop=True).then_inc(s_n, 1)

                    def step(it, k, first):
                        gates(it, k)
                        if not first:
                            transpose_rows((k - 1) % SLOTS, it * SLOTS + (k + (layer + 1) * CHUNKS - 1))

                    steps(pe, CITER, step)
                    transpose_rows(SLOTS - 1, (layer + 2) * CHUNKS - 1)

            @block.scalar
            def _(act):
                n = 0
                for to in (dstT[:, :], relT[:, :], srcT[:, :]):
                    for g in range(TQ):
                        act.wait_ge(s_eT, n + 1)
                        nc.scalar.copy(by_g(to)[:, g, :], sums[n % 2][:, 0:QR]).then_inc(s_eC, 1)
                        n += 1
                for layer in range(LAYERS):
                    act.wait_ge(s_comb, layer + 1)
                    t = nc.scalar.copy(comb[:, layer, :], sums[layer][:, 0:3 * P])
                t.then_inc(s_combC, 1)
                for c in range(UC):
                    act.wait_ge(s_uT, c + 1)
                    for half, to in enumerate((key_units, slo_units)):
                        nc.scalar.copy(to[:, :, c * P:(c + 1) * P],
                                       sums[c % 2][:, half * UT * P:(half + 1) * UT * P].rearrange("p (i q) -> p i q", i=UT)
                                       ).then_inc(s_uC, 1)

                def rows_hi(it, k, u, stage):
                    act.wait_ge(s_rT, u + 1)
                    wait_past(act, s_rS[k], (it + stage * CITER) * 16)
                    nc.scalar.copy(part_of(k, 0), ps_rows[0:CP, :].rearrange("p (j n) -> p j n", j=CJ)).then_inc(s_hi, 1)

                def rows_mid(k, u):
                    act.wait_ge(s_rest, u + 1)
                    nc.scalar.copy(part_of(k, 1), rest.rearrange("p (j n) -> p j n", j=CJ)).then_inc(s_mid, 1)

                def linear_step(it, k, first):
                    c = it * SLOTS + k
                    before = (k - 1) % SLOTS
                    act.wait_ge(s_var, c + 1)
                    nc.scalar.activation(rstd[:, :], mv[:, :, 1], ACT.Sqrt, bias=eps_t[0:CP, :]).then_inc(s_std, 1)
                    act.wait_ge(s_lnT, c + 1)
                    wait_past(act, s_lin, c)
                    nc.scalar.activation(lnT.rearrange("f (p j) -> f j p", j=CJ),
                                         ps_ln[:, 0:CH].rearrange("f (j p) -> f j p", j=CJ), ACT.Relu).then_inc(s_lnC, 1)
                    if not first:
                        rows_hi(it - (k == 0) if k else it - 1, before, c - 1, 0)
                        rows_mid(before, c - 1)
                    act.wait_ge(s_lin, c + 1)
                    wait_past(act, s_kS[k], it * 16)
                    if not (isinstance(it, int) and it == 0):
                        act.wait_ge(s_rT, c - SLOTS + 1)
                    nc.scalar.activation(hs[:, k, :], ps_lin[:, 0:CH], ACT.Identity, bias=lin_bias[:, :]).then_inc(s_h0, 1)

                steps(act, CITER, linear_step)
                rows_hi(CITER - 1, SLOTS - 1, CHUNKS - 1, 0)
                rows_mid(SLOTS - 1, CHUNKS - 1)
                act.wait_ge(s_wide, 1)
                wide = act.value_load(wide_i[0:1, 0:1], min_val=0, max_val=1)

                def hand_indices(it, u, k):
                    wait_past(act, s_got[k], u * (16 * TG))
                    nc.scalar.copy(idx[:, k, :], srcT[:, bass.ds((it * SLOTS + k) * TG, TG)]).then_inc(s_idx, 1)

                act.wait_ge(s_strips, 1)
                for k in range(SLOTS):
                    act.wait_ge(s_kS[k], 16 * CITER)
                act.sem_inc(s_winfree, 2)
                act.sem_inc(s_evac, 2)
                with act.Fori(0, DWINS // 2) as i:
                    for o in range(2):
                        w = i * 2 + o
                        act.wait_ge(s_winfree, w + 1)
                        to = win_bufs[o].rearrange("p (b d) -> p d b", b=BLOCKS)
                        for m in range(PAIRS):
                            act.wait_ge(s_bsum, w * PAIRS + (m + OB + 1))
                            nc.scalar.copy(to[:, m * 2 * SUB:(m + 1) * 2 * SUB, :].rearrange("p (u d) b -> p u d b", u=2),
                                           pair[m % 2][:, :].rearrange("p (u n) -> p u n", u=2)[:, :, 0:SW].rearrange(
                                               "p u (d b) -> p u d b", b=BLOCKS)).then_inc(s_evac, 1)

                skip, kept = load_skip(act)
                last, more = load_last(act)
                for layer in range(LAYERS):
                    past = kept * layer if layer else 0

                    def hand(i, k):
                        hand_indices(iteration(skip, i), past + i, k)

                    def hand_ahead(i, k):
                        k += AHEAD
                        hand(i + k // SLOTS, k % SLOTS)

                    with act.If(wide):
                        iterations(act, GITER, lambda i: [hand(i, k) for k in range(SLOTS)], peel=True)
                    with act.Else():
                        for k in range(AHEAD):
                            hand(0, k)

                        def dense_step(d):
                            for s in range(ITERS * SLOTS):
                                hand_ahead(d * ITERS + s // SLOTS, s % SLOTS)

                        iterations(act, DLOOPS, dense_step, peel=True)
                        with act.If(more):
                            with act.Fori(DITER, last) as i:
                                for k in range(SLOTS):
                                    hand_ahead(i, k)
                        for k in range(AHEAD, SLOTS):
                            hand(last, k)

                    def step(it, k, first):
                        c = it * SLOTS + k
                        v = c + layer * CHUNKS
                        before = (k - 1) % SLOTS
                        publish = not first and layer < LAYERS - 1
                        act.wait_ge(s_rz, v + 1)
                        act.wait_ge(s_h0, v + CHUNKS)
                        nc.scalar.activation(gr, ps_r[:, 0:CH], ACT.Sigmoid, bias=brz[:, 0:1])
                        nc.scalar.activation(gz, ps_z[:, 0:CH], ACT.Sigmoid, bias=brz[:, 1:2]).then_inc(s_rzread, 1)
                        if publish:
                            rows_hi(it - (k == 0), before, v + (CHUNKS - 1), layer + 1)
                        act.wait_ge(s_nread, v + 1)
                        nc.scalar.activation(cand, npre, ACT.Tanh, bias=bih[:, 2:3]).then_inc(s_cand, 1)
                        if publish:
                            rows_mid(before, v + (CHUNKS - 1))

                    steps(act, CITER, step)
                    if layer < LAYERS - 1:
                        rows_hi(CITER - 1, SLOTS - 1, (layer + 2) * CHUNKS - 1, layer + 1)
                        rows_mid(SLOTS - 1, (layer + 2) * CHUNKS - 1)

            @block.vector
            def _(dve):
                done = [0]

                def then(ins):
                    done[0] += 1
                    ins.then_inc(s_dve, 1)
                    dve.wait_ge(s_dve, done[0])

                dve.sem_inc(s_taken, 2)
                dve.sem_inc(s_xused, SLOTS)
                dve.wait_ge(s_dst, 16)
                nc.vector.tensor_copy(dst_f, dst_rows).then_inc(s_dstf, 1)
                dve.wait_ge(s_dstf, 1)
                tiled = dst_f.rearrange("q (g n) -> q g n", n=P)
                nc.vector.tensor_reduce(tmin[:, :], tiled, AX.X, ALU.min).then_inc(s_min, 1)
                then(nc.vector.tensor_reduce(tmax[:, :], tiled, AX.X, ALU.max))
                dve.wait_ge(s_min, 1)
                then(nc.vector.tensor_reduce(lo[:, :], tmin[:, :].rearrange("q (g t) -> q g t", t=TG), AX.X, ALU.min))
                then(nc.vector.tensor_reduce(hi[:, :], tmax[:, :].rearrange("q (g t) -> q g t", t=TG), AX.X, ALU.max))
                nc.vector.tensor_copy(lo_i[:, :], lo[:, :]).then_inc(s_lo, 1)
                nc.vector.tensor_tensor(rel_f.rearrange("q (g n) -> q g n", n=TG * P),
                                        dst_f.rearrange("q (g n) -> q g n", n=TG * P),
                                        lo[:, :].unsqueeze(2).broadcast_to([QR, GQ, TG * P]),
                                        ALU.subtract).then_inc(s_rel, 1)
                then(nc.vector.tensor_tensor(hi[:, :], hi[:, :], lo[:, :], ALU.subtract))
                then(nc.vector.tensor_reduce(checks[:, 0:1], hi[:, :], AX.X, ALU.max))
                dve.wait_ge(s_src, 16)
                nc.vector.tensor_copy(src_f, src_rows).then_inc(s_srcf, 1)
                then(nc.vector.tensor_scalar(key_f.bitcast(i32), src_rows, 7, None, ALU.arith_shift_right))
                then(nc.vector.tensor_copy(slo_f, key_f.bitcast(i32)))
                nc.vector.scalar_tensor_tensor(out=key_f, in0=dst_f, scalar=float(BLOCKS), in1=slo_f, op0=ALU.mult,
                                               op1=ALU.add).then_inc(s_key, 1)
                dve.wait_ge(s_key, 1)
                dve.wait_ge(s_srcf, 1)
                nc.vector.scalar_tensor_tensor(out=slo_f, in0=slo_f, scalar=-float(P), in1=src_f, op0=ALU.mult,
                                               op1=ALU.add).then_inc(s_slo, 1)
                dve.wait_ge(s_next, 16)
                then(nc.vector.tensor_tensor(tnext, tmax[:, :], tnext, ALU.is_gt))
                then(nc.vector.tensor_reduce(checks[:, 1:2], tnext, AX.X, ALU.max))
                nc.vector.tensor_scalar(checks[:, 0:1], checks[:, 0:1], float(WIN), None, ALU.is_ge).then_inc(s_chk, 1)
                dve.wait_ge(s_const, 8)
                for i in range(STRIPS // THR_STEP):
                    at = below.rearrange("q (s g) -> q s g", g=TQ)
                    n = slice(i * THR_STEP, (i + 1) * THR_STEP)
                    then(nc.vector.tensor_tensor(at, tmin[:, :].unsqueeze(1).broadcast_to([QR, THR_STEP, TQ]),
                                                 scratch[0:QR, n].unsqueeze(2).broadcast_to([QR, THR_STEP, TQ]), ALU.is_lt))
                    nc.vector.tensor_reduce(cnt[:, n], at, AX.X, ALU.add).then_inc(s_cnt, 1)
                    dve.wait_ge(s_cnt, i + 1)
                dve.wait_ge(s_chkP, 1)
                nc.vector.tensor_scalar(wide_i[:, :], ps_misc[0:1, 0:1], 0.0, None, ALU.is_gt).then_inc(s_wide, 1)
                then(nc.vector.tensor_reduce(ok_b, ps_misc[:, 0:2], AX.X, ALU.max))
                then(nc.vector.tensor_scalar(ok_b, ok_b, 0.0, None, ALU.is_le))
                dve.wait_ge(s_cntP, 1)
                dve.wait_ge(s_eC, 3 * TQ)
                starts, units_of = reach
                w = STRIPS // SPL
                for i in range(SPL):
                    t = nc.vector.tensor_scalar(starts[:, i * w:(i + 1) * w], banks4[i][:, 0:w], 1.0, None, ALU.max)
                    t.then_inc(s_strips if i == SPL - 1 else s_dve, 1)
                done[0] += SPL - 1
                dve.wait_ge(s_strips, 1)
                dve.wait_ge(s_dve, done[0])
                then(nc.vector.tensor_scalar(delta[:, 0:1], starts[:, 0:1], 1.0, None, ALU.subtract))
                then(nc.vector.tensor_tensor(delta[:, 1:STRIPS], starts[:, 1:STRIPS], starts[:, 0:STRIPS - 1], ALU.subtract))
                whole = scratch.bitcast(i32)
                then(nc.vector.tensor_scalar(whole, delta, 2.0, None, ALU.add))
                then(nc.vector.tensor_scalar(whole, whole, 1, None, ALU.arith_shift_right))
                then(nc.vector.tensor_copy(units_of, whole))
                then(nc.vector.scalar_tensor_tensor(out=code, in0=units_of, scalar=-float(UT), in1=delta, op0=ALU.mult,
                                                    op1=ALU.add))
                then(nc.vector.tensor_scalar(code, code, float(BIG), None, ALU.add))
                now, step_, n = 1, 1, STRIPS
                while step_ < n:
                    a, b = reach[now], reach[1 - now]
                    then(nc.vector.tensor_copy(b[:, 0:step_], a[:, 0:step_]))
                    then(nc.vector.tensor_tensor(b[:, step_:n], a[:, step_:n], a[:, 0:n - step_], ALU.add))
                    now, step_ = 1 - now, step_ * 2
                upto = reach[now]
                for c in range(UC):
                    then(nc.vector.scalar_tensor_tensor(out=scratch, in0=upto, scalar=unit_no[:, c:c + 1], in1=code,
                                                        op0=ALU.is_le, op1=ALU.mult))
                    then(nc.vector.tensor_reduce(unit_sum[:, c:c + 1], scratch, AX.X, ALU.add))
                then(nc.vector.tensor_scalar(scratch, upto, float(UNITS), None, ALU.is_le))
                then(nc.vector.tensor_reduce(reached, scratch, AX.X, ALU.add))
                then(nc.vector.scalar_tensor_tensor(out=scratch, in0=upto, scalar=float(UNITS), in1=delta,
                                                    op0=ALU.is_le, op1=ALU.mult))
                then(nc.vector.tensor_reduce(spared, scratch, AX.X, ALU.add))
                then(nc.vector.tensor_scalar(ulist_i[:, :], unit_sum, float(BIG - 1), None, ALU.add))
                then(nc.vector.tensor_scalar(ulist_i[:, :], ulist_i[:, :], BIG.bit_length() - 1, None,
                                             ALU.arith_shift_right))
                then(nc.vector.tensor_copy(unit_strip, ulist_i[:, :]))
                then(nc.vector.scalar_tensor_tensor(out=unit_tile, in0=unit_strip, scalar=-float(BIG), in1=unit_sum,
                                                    op0=ALU.mult, op1=ALU.add))
                then(nc.vector.scalar_tensor_tensor(out=unit_tile, in0=unit_no, scalar=float(UT), in1=unit_tile,
                                                    op0=ALU.mult, op1=ALU.add))
                then(nc.vector.tensor_scalar(unit_live, unit_strip, reached, ok_b, ALU.is_lt, ALU.mult))
                for i in range(UT):
                    then(nc.vector.tensor_scalar(unit_sum, unit_tile, float(TILES - i), None, ALU.subtract))
                    then(nc.vector.tensor_tensor(unit_sum, unit_sum, unit_live, ALU.mult))
                    then(nc.vector.tensor_scalar(unit_idx[:, :, i], unit_sum, float(TILES), None, ALU.add))
                    then(nc.vector.tensor_scalar(unit_shift[:, :, i], unit_strip, float(SW), None, ALU.mult))
                dve.sem_inc(s_uidx, 1)
                then(nc.vector.tensor_scalar(limit_b, reached, float(SUB), ok_b, ALU.mult, ALU.mult))
                then(nc.vector.tensor_scalar(spared, spared, 5243.0, None, ALU.mult))
                then(nc.vector.tensor_copy(skip_i[:, 0:1], spared[0:1, :]))
                then(nc.vector.tensor_scalar(skip_i[:, 0:1], skip_i[:, 0:1], 17, None, ALU.arith_shift_right))
                then(nc.vector.tensor_copy(spared[0:1, :], skip_i[:, 0:1]))
                then(nc.vector.tensor_scalar(spared[0:1, :], spared[0:1, :], float(GITER - DITER - 1), ok_b[0:1, :],
                                             ALU.min, ALU.mult))
                then(nc.vector.tensor_copy(skip_i[:, 0:1], spared[0:1, :]))
                then(nc.vector.tensor_scalar(skip_i[:, 3:4], spared[0:1, :], -1.0, float(GITER - DITER - 1), ALU.mult, ALU.add))
                then(nc.vector.tensor_scalar(skip_i[:, 2:3], spared[0:1, :], -1.0, float(GITER - 1), ALU.mult, ALU.add))
                nc.vector.tensor_scalar(skip_i[:, 1:2], spared[0:1, :], -1.0, float(GITER), ALU.mult,
                                        ALU.add).then_inc(s_steer, 1)
                dve.wait_ge(s_bases, 16)
                then(nc.vector.tensor_scalar(bases[:, :], bases[:, :], limit_b[0:1, :], None, ALU.max))
                dve.wait_ge(s_lob, 16)
                then(nc.vector.tensor_scalar(lo_b, lo_b, -1.0, limit_b, ALU.mult, ALU.add))
                then(nc.vector.tensor_scalar(lo_b, lo_b, 0.0, None, ALU.max))
                by_group = relT[:, :].rearrange("p (g t) -> p g t", t=TG)
                then(nc.vector.tensor_tensor(by_group, by_group, lo_b.unsqueeze(2).broadcast_to([P, GROUPS, TG]),
                                             ALU.subtract))
                first = ulist_i[:, 0:1]
                then(nc.vector.tensor_copy(first, unit_no[:, 0:1]))
                then(nc.vector.tensor_scalar(first, first, SUB.bit_length() - 1, None, ALU.arith_shift_right))
                then(nc.vector.tensor_copy(digit, first))
                then(nc.vector.scalar_tensor_tensor(out=digit, in0=digit, scalar=-float(SUB), in1=unit_no[:, 0:1],
                                                    op0=ALU.mult, op1=ALU.add))
                for k in range(P // PER):
                    if k:
                        dve.wait_ge(s_relP, k)
                    nc.vector.tensor_tensor(select[:, :].rearrange("p (u d) -> p u d", d=SUB),
                                            ident[:, k * PER:(k + 1) * PER].unsqueeze(2).broadcast_to([P, PER, SUB]),
                                            ident[:, k * PER:k * PER + 1].unsqueeze(2).broadcast_to([P, PER, SUB]),
                                            ALU.subtract).then_inc(s_relm, 1)
                dve.wait_ge(s_ugot, 16 * UC * UT)
                keys = gathered.rearrange("p (t n) -> p t n", n=2 * P)[:, :, 0:P]
                nc.vector.tensor_tensor(keys, keys, unit_shift[:, :, :].rearrange("p c i -> p (c i)").unsqueeze(2)
                                        .broadcast_to([P, UC * UT, P]), ALU.subtract).then_inc(s_ushift, 1)
                dve.wait_ge(s_relP, P // PER)
                K = P // PER
                nc.vector.tensor_scalar(relcol[:, :].rearrange("p (c k) -> p k c", k=K),
                                        ps_misc[:, 0:K * UC].rearrange("p (k c) -> p k c", k=K), float(SUB), digit,
                                        ALU.mult, ALU.add).then_inc(s_relC, 1)
                nc.vector.tensor_scalar(dbases[:, :].rearrange("p (c k) -> p k c", k=K),
                                        ps_misc[0:1, K * UC:2 * K * UC].rearrange("p (k c) -> p k c", k=K), float(SUB), None,
                                        ALU.mult).then_inc(s_relC, 1)
                dve.wait_ge(s_relC, 2)
                dve.wait_ge(s_w, 16 * 7)
                nc.vector.tensor_tensor(brz[:, :], bih[:, 0:2], bhh[:, 0:2], ALU.add).then_inc(s_dve, 1)
                done[0] += 1

                def rows_rest(u):
                    dve.wait_ge(s_hi, u + 1)
                    wait_past(dve, s_rC, u)
                    nc.vector.tensor_tensor(rest.rearrange("p (j n) -> p j n", j=CJ),
                                            ps_rows[0:CP, :].rearrange("p (j n) -> p j n", j=CJ), part_of(u_slot[0], 0),
                                            ALU.subtract).then_inc(s_rest, 1)

                def rows_lo(u):
                    dve.wait_ge(s_mid, u + 1)
                    nc.vector.tensor_tensor(part_of(u_slot[0], 2), rest.rearrange("p (j n) -> p j n", j=CJ),
                                            part_of(u_slot[0], 1), ALU.subtract).then_inc(s_rC, 1)

                def norm_step(it, k, first):
                    c = it * SLOTS + k
                    dve.wait_ge(s_xload[k], (it + 1) * 16)
                    wait_past(dve, s_xn, c)
                    for j in range(CJ):
                        t = nc.vector.bn_stats(stats[:, j, :], xrow[:, k, j * P:(j + 1) * P])
                    t.then_inc(s_stats, 1)
                    dve.wait_ge(s_stats, c * 2 + 1)
                    dve.sem_inc(s_passed, 1)
                    for j in range(CJ):
                        t = nc.vector.bn_aggr(mv[:, j, :], stats[:, j, :])
                    t.then_inc(s_var, 1)
                    dve.wait_ge(s_var, c + 1)
                    dve.wait_ge(s_std, c + 1)
                    nc.vector.reciprocal(rstd[:, :], rstd[:, :]).then_inc(s_stats, 1)
                    dve.wait_ge(s_stats, c * 2 + 2)
                    wait_past(dve, s_lnT, c)
                    for j in range(CJ):
                        t = nc.vector.tensor_scalar(xn[:, j * P:(j + 1) * P], xrow[:, k, j * P:(j + 1) * P],
                                                    mv[:, j, 0:1], rstd[:, j:j + 1], ALU.subtract, ALU.mult)
                    t.then_inc(s_xn, 1)
                    dve.wait_ge(s_xn, c + 1)
                    dve.sem_inc(s_xused, 1)
                    if not first:
                        u_slot[0] = (k - 1) % SLOTS
                        rows_rest(c - 1)
                        rows_lo(c - 1)

                steps(dve, CITER, norm_step)
                u_slot[0] = SLOTS - 1
                rows_rest(CHUNKS - 1)
                rows_lo(CHUNKS - 1)

                dve.wait_ge(s_combC, 1)
                wide = dve.value_load(wide_i[0:1, 0:1], min_val=0, max_val=1)

                def group_onehot(it, u, k):
                    dve.wait_ge(s_sum, u * SLOTS + (k + 1))
                    nc.vector.tensor_tensor(
                        onehot[:, k, :].rearrange("p (t n) -> p t n", t=TG),
                        iota_b[:, :].unsqueeze(1).broadcast_to([P, TG, WIN]),
                        relT[:, bass.ds((it * SLOTS + k) * TG, TG)].unsqueeze(2).broadcast_to([P, TG, WIN]),
                        ALU.is_equal).then_inc(s_oh, 1)

                def group_add(it, u, k):
                    n = u * SLOTS + k
                    base = dve.value_load(bases[0:1, bass.ds(it * SLOTS + k, 1)], min_val=0, max_val=NODES - 1)
                    dve.wait_ge(s_sum, n + (SLOTS + 1))
                    dve.wait_ge(s_taken, n + 2)
                    at = aggT[:, bass.ds(base, WIN)]
                    nc.vector.tensor_tensor(at, at, sums[BANK[k]][:, 0:WIN], ALU.add).then_inc(s_taken, 1)

                def dense_add(j, w, groups):
                    base = dve.value_load(dbases[0:1, bass.ds(j, 1)], min_val=0, max_val=STRIPS * SUB)
                    dve.wait_ge(s_taken, groups + 2)
                    dve.wait_ge(s_dT, w + 1)
                    at = aggT[:, bass.ds(base, P)]
                    nc.vector.tensor_tensor(at, at, ps_denseT, ALU.add).then_inc(s_dadd, 1)
                    dve.wait_ge(s_dadd, w + 1)

                def dense_sum(a, w):
                    dve.wait_ge(s_used[PIECES - 1], w + 1)
                    nc.vector.tensor_copy(dsum[:, :], ps_dense[a % 2][:, 2 * P:3 * P]).then_inc(s_dpart, 1)
                    for part in (1, 0):
                        dve.wait_ge(s_dpart, w * 2 + (2 - part))
                        nc.vector.tensor_tensor(dsum[:, :], dsum[:, :], ps_dense[a % 2][:, part * P:(part + 1) * P],
                                                ALU.add).then_inc(s_dpart if part else s_dcopy, 1)

                def make_select(j):
                    nc.vector.tensor_scalar(select[:, :], iota_b[:, :], relcol[:, bass.ds(j, 1)], None,
                                            ALU.is_equal).then_inc(s_sel, 1)

                def slow_groups(layer):
                    with dve.Fori(0, GROUPS) as g:
                        nc.vector.tensor_copy(shifted[:, :], dstT[:, bass.ds(g * TG, TG)]).then_inc(s_sh, 1)
                        with dve.Fori(0, SWINS) as w:
                            m = (g + layer * GROUPS) * SWINS + w
                            dve.wait_ge(s_sh, m + (g + layer * GROUPS) + 1)
                            nc.vector.tensor_tensor(
                                onehot_slow, iota_s[:, :].unsqueeze(1).broadcast_to([P, TG, SWIN]),
                                shifted[:, :].unsqueeze(2).broadcast_to([P, TG, SWIN]),
                                ALU.is_equal).then_inc(s_slow_oh, 1)
                            dve.wait_ge(s_slow_oh, m + 1)
                            nc.vector.tensor_scalar(shifted[:, :], shifted[:, :], float(SWIN), None,
                                                    ALU.subtract).then_inc(s_sh, 1)
                            dve.wait_ge(s_slow_sum, m + 1)
                            at = aggT[:, bass.ds(w * SWIN, SWIN)]
                            nc.vector.tensor_tensor(at, at, sums[0][:, 0:SWIN], ALU.add).then_inc(s_slow_add, 1)
                            dve.wait_ge(s_slow_add, m + 1)
                        dve.wait_ge(s_sh, (g + (layer * GROUPS + 1)) * (SWINS + 1))

                dve.wait_ge(s_uC, 2 * UC)
                dve.sem_inc(s_boh, 1)
                dve.sem_inc(s_bol, PAIRS)
                with dve.Fori(0, DWINS // 2) as i:
                    for o in range(2):
                        w = i * 2 + o
                        dve.wait_ge(s_bol, (w + 1) * (PAIRS // 2))
                        nc.vector.tensor_copy(sw[:, o, :], sloT[:, bass.ds(w * (PER * UT), PER * UT)]).then_inc(s_sw, 1)
                        dve.wait_ge(s_boh, w * PAIRS + 1)
                        nc.vector.tensor_copy(kw, keyT[:, bass.ds(w * (PER * UT), PER * UT)]).then_inc(s_kw, 1)
                        dve.wait_ge(s_kw, w + 1)
                        dve.wait_ge(s_sw, w + 1)
                        for m in range(PAIRS):
                            if m % 2 == 0:
                                dve.wait_ge(s_bsum, w * PAIRS + (m + 2))
                                for t in range(ON_VECTOR):
                                    at = m * 2 * UT + t
                                    nc.vector.tensor_scalar(olv[:, m // 2 % 2, t, :], iota_b[:, :], sw[:, o, at:at + 1],
                                                            None, ALU.is_equal)
                            else:
                                dve.wait_ge(s_bsum, w * PAIRS + (m + 1))
                            for t in range(2 * UT):
                                ins = nc.vector.tensor_scalar(ohv[:, m % OB, t, :], iota_w,
                                                              kw[:, m * 2 * UT + t:m * 2 * UT + t + 1], None, ALU.is_equal)
                            ins.then_inc(s_boh, 1)
                dve.wait_ge(s_aS, 16 * DWINS)
                skip, kept = load_skip(dve)
                last, more = load_last(dve)
                for layer in range(LAYERS):
                    nc.vector.memset(aggT[:, :], 0.0).then_inc(s_zero, 1)
                    dve.wait_ge(s_zero, layer + 1)
                    with dve.If(wide):
                        slow_groups(layer)
                    with dve.Else():
                        past = kept * layer if layer else 0

                        def make_onehot(i, k):
                            i, k = i + k // SLOTS, k % SLOTS
                            group_onehot(iteration(skip, i), past + i, k)

                        def group(i, k):
                            make_onehot(i, k + 1)
                            group_add(iteration(skip, i), past + i, k)

                        def dense_step(d):
                            if isinstance(d, int):
                                make_select(0)
                            for s in range(ITERS * SLOTS):
                                i, k = d * ITERS + s // SLOTS, s % SLOTS
                                group(i, k)
                                for what, a in ends_in(s):
                                    w = d * BODY + (a + layer * DWINS)
                                    if what == "sum":
                                        dense_sum(a, w)
                                    elif a >= 0 or not isinstance(d, int):
                                        dense_add(d * BODY + a, w, (past + i) * SLOTS + (k + 1))
                                        make_select(d * BODY + (a + 1))

                        make_onehot(0, 0)
                        iterations(dve, DLOOPS, dense_step, peel=True)
                        dense_add(DWINS - 1, (layer + 1) * DWINS - 1, (past + DITER) * SLOTS)
                        with dve.If(more):
                            with dve.Fori(DITER, last) as i:
                                for k in range(SLOTS):
                                    group(i, k)
                        for k in range(SLOTS):
                            if k < SLOTS - 1:
                                group(last, k)
                            else:
                                group_add(iteration(skip, last), past + last, k)
                        dve.wait_ge(s_taken, (past + kept) * SLOTS + 2)
                        dve.sem_inc(s_passed, 1)
                    dve.sem_inc(s_agg, 1)

                    def add_rows(it, k, u):
                        dve.wait_ge(s_rT, u + 1)
                        dve.wait_ge(s_xload[k], (it + (CITER + 1)) * 16)
                        dve.wait_ge(s_rS[k], (it + LAYERS * CITER) * 16)
                        nc.vector.tensor_tensor(hrow_f[:, k, 0:CJ * P], ps_rows[0:CP, :], xrow[:, k, :],
                                                ALU.add).then_inc(s_rC, 1)
                        dve.wait_ge(s_rC, u + 1)
                        dve.sem_inc(s_rest, 1)
                        dve.sem_inc(s_xused, 1)

                    def step(it, k, first):
                        c = it * SLOTS + k
                        v = c + layer * CHUNKS
                        h = hs[:, k, :]
                        before = (k - 1) % SLOTS
                        u_slot[0] = before
                        dve.wait_ge(s_n, v + 1)
                        dve.wait_ge(s_rzread, v + 1)
                        wait_past(dve, s_cand, v)
                        nc.vector.scalar_tensor_tensor(out=npre, in0=ps_hn[:, 0:CH], scalar=bhh[:, 2:3],
                                                       in1=gr, op0=ALU.add, op1=ALU.mult).then_inc(s_t1, 1)
                        dve.wait_ge(s_t1, v + 1)
                        nc.vector.tensor_tensor(npre, npre, ps_in[:, 0:CH], ALU.add).then_inc(s_nread, 1)
                        if not first:
                            if layer == LAYERS - 1:
                                add_rows(it - (k == 0), before, v + (CHUNKS - 1))
                            else:
                                rows_rest(v + (CHUNKS - 1))
                        dve.wait_ge(s_cand, v + 1)
                        nc.vector.tensor_tensor(diff, h, cand, ALU.subtract).then_inc(s_d, 1)
                        dve.wait_ge(s_d, v * 2 + 1)
                        nc.vector.tensor_tensor(diff, diff, gz, ALU.mult).then_inc(s_d, 1)
                        dve.wait_ge(s_d, v * 2 + 2)
                        nc.vector.tensor_tensor(h, diff, cand, ALU.add).then_inc(s_h0, 1)
                        dve.wait_ge(s_h0, v + (CHUNKS + 1))
                        if not first and layer < LAYERS - 1:
                            rows_lo(v + (CHUNKS - 1))

                    steps(dve, CITER, step)
                    u_slot[0] = SLOTS - 1
                    if layer == LAYERS - 1:
                        add_rows(CITER - 1, SLOTS - 1, (layer + 2) * CHUNKS - 1)
                    else:
                        rows_rest((layer + 2) * CHUNKS - 1)
                        rows_lo((layer + 2) * CHUNKS - 1)


def kernel(x, src, dst, L0_gnn_lin_w, L0_gnn_lin_b, L0_gnn_weight, L0_gnn_w_ih, L0_gnn_w_hh, L0_gnn_b_ih, L0_gnn_b_hh):
    import numpy as np
    import concourse.bacc as bacc
    from concourse import mybir as mb
    from concourse.bass_utils import run_bass_kernel_spmd

    arrays = {
        "x": np.asarray(x), "src": np.asarray(src), "dst": np.asarray(dst),
        "lin_wT": np.asarray(L0_gnn_lin_w).T, "lin_b": np.asarray(L0_gnn_lin_b),
        "weightT": np.asarray(L0_gnn_weight).transpose(0, 2, 1), "w_ihT": np.asarray(L0_gnn_w_ih).T,
        "w_hhT": np.asarray(L0_gnn_w_hh).T, "b_ih": np.asarray(L0_gnn_b_ih), "b_hh": np.asarray(L0_gnn_b_hh),
    }
    arrays = {f"in_{k}": np.ascontiguousarray(v) for k, v in arrays.items()}
    nc = bacc.Bacc("TRN2", target_bir_lowering=False, num_devices=1)
    args = [nc.dram_tensor(k, v.shape, mb.dt.from_np(v.dtype), kind="ExternalInput").ap() for k, v in arrays.items()]
    shape = arrays["in_x"].shape
    out = nc.dram_tensor("out", shape, mb.dt.float32, kind="ExternalOutput").ap()
    build(nc, *args, out, NODES=shape[0], EDGES=arrays["in_src"].shape[0], LAYERS=arrays["in_weightT"].shape[0])
    r = run_bass_kernel_spmd(nc, [arrays], core_ids=[0])
    return r.results[0]["out"]
```

```python
import concourse.bass as bass
from concourse import mybir
from contextlib import ExitStack


def build(nc, x, src, dst, lin_wT, lin_b, weightT, w_ihT, w_hhT, b_ih, b_hh, out, NODES, EDGES, LAYERS):
    fp32 = mybir.dt.float32
    bf16 = mybir.dt.bfloat16
    fp16 = mybir.dt.float16
    i32 = mybir.dt.int32
    i16 = mybir.dt.int16
    ALU = mybir.AluOpType
    ACT = mybir.ActivationFunctionType
    AX = mybir.AxisListType

    P = 128
    PARTS = 3
    TILES = EDGES // P
    TG = 5
    GROUPS = TILES // TG
    SLOTS = 5
    GITER = GROUPS // SLOTS
    QR = 125
    TQ = TILES // QR
    GQ = TQ // TG
    WIN = 128
    SWIN = 512
    SWINS = -(-NODES // SWIN)
    CH = 500
    CP = 125
    CJ = CH // CP
    CHUNKS = NODES // CH
    CITER = CHUNKS // SLOTS
    BLOCKS = -(-NODES // P)
    SUB = 4
    SW = SUB * BLOCKS
    UT = 2
    DWINS = 60
    PER = P // SUB
    UNITS = DWINS * PER
    UC = UNITS // P
    STRIPS = UNITS
    SPL = 4
    RATES = ((12, 3, 2), (6, 4, 3))
    DITER = sum(n * iters for n, _, iters in RATES)
    LATER = 16
    OB = 4
    PAIRS = PER // 2
    ON_VECTOR = 3
    ON_SCALAR = ON_VECTOR
    PIECES = 7
    BIG = 4096
    AHEAD = 3
    AGGW = max(SWINS * SWIN, NODES + WIN, 4 * TQ * P)
    EPS = 1e-5
    assert 2 * STRIPS < BIG and STRIPS * SUB + P <= NODES and UNITS % P == 0 and PAIRS % OB == 0 and DWINS % 2 == 0
    assert UT == 2 and UNITS * BIG < 2 ** 24 and sum(n * body for n, body, _ in RATES) == DWINS
    assert TILES * P == EDGES and GITER * SLOTS * TG == TILES and TQ * QR == TILES
    assert CITER * SLOTS * CH == NODES and TQ % TG == 0

    ctx = ExitStack()
    with ctx:
        def sb(name, shape, dt=fp32):
            return ctx.enter_context(nc.sbuf_tensor(name, shape, dt))

        def sem(name):
            return ctx.enter_context(nc.semaphore(name))

        def sems(name, n=SLOTS):
            return [sem(f"{name}{k}") for k in range(n)]

        def dram(name, shape, dt):
            return nc.dram_tensor(name, shape, dt, kind="Internal").ap()

        table = dram("table", [BLOCKS * P, PARTS * P], bf16)
        state = dram("state", [P, NODES], fp32)
        counts = dram("counts", [DWINS, P, BLOCKS * P], bf16)
        bases_dram = dram("bases_dram", [QR, GQ], i32)
        lows_dram = dram("lows_dram", [QR, GQ], fp32)
        mins_dram = dram("mins_dram", [QR + 1, TQ], fp32)
        edge_rows = dram("edge_rows", [TILES + 1, 2 * P], fp32)

        aggT = sb("aggT", [P, AGGW])
        srcT = sb("srcT", [P, TILES], i16)
        dstT = sb("dstT", [P, TILES], i16)
        relT = sb("relT", [P, TILES], bf16)
        idx = sb("idx", [P, SLOTS, TG], i32)
        iota_b = sb("iota_b", [P, WIN], bf16)
        iota_s = sb("iota_s", [P, SWIN])
        shifted = sb("shifted", [P, TG])
        ident = sb("ident", [P, P])
        ones = sb("ones", [P, P], bf16)
        one = sb("one", [P, 1])
        bases = sb("bases", [1, GROUPS], i32)
        wide_i = sb("wide_i", [1, 1], i32)
        skip_i = sb("skip_i", [1, 4], i32)
        verdict = sb("verdict", [P, 8])
        ok_b, limit_b, reached, spared = (verdict[:, i:i + 1] for i in range(4))
        digit = verdict[:, 4:5]
        ulist = sb("ulist", [P, 5, UC])
        unit_no, unit_sum, unit_strip, unit_tile, unit_live = (ulist[:, i, :] for i in range(5))
        ulist_i = sb("ulist_i", [P, UC], i32)
        unit_idx = sb("unit_idx", [P, UC, UT], i32)
        unit_shift = sb("unit_shift", [P, UC, UT])
        relcol = sb("relcol", [P, DWINS])
        dbases = sb("dbases", [1, DWINS], i32)
        select = sb("select", [P, P])
        whh_sb = sb("whh_sb", [P, 3 * P])
        comb = sb("comb", [P, LAYERS, 3 * P])
        lin_sb = sb("lin_sb", [P, P])
        lin_bias = sb("lin_bias", [P, 1])
        bih = sb("bih", [P, 3])
        bhh = sb("bhh", [P, 3])
        brz = sb("brz", [P, 2])
        eps_t = sb("eps_t", [P, 1])
        stats = sb("stats", [CP, CJ, 6])
        mv = sb("mv", [CP, CJ, 2])
        rstd = sb("rstd", [CP, CJ])
        dsum = sb("dsum", [P, P])
        tmin = sb("tmin", [QR, TQ])
        tmax = sb("tmax", [QR, TQ])
        big = sb("big", [1, TQ])
        lo = sb("lo", [QR, GQ])
        hi = sb("hi", [QR, GQ])
        lo_i = sb("lo_i", [QR, GQ], i32)
        checks = sb("checks", [QR, 2])
        faults = sb("faults", [QR, 2], bf16)
        tstrip = sb("tstrip", [QR, TQ])
        tmin_i = sb("tmin_i", [QR, TQ], i32)

        def carve(tensor, wanted):
            at, found = 0, {}
            for name, (n, dt) in wanted.items():
                k = n * (2 if dt in (fp32, i32) else 1)
                v = tensor[:, at:at + k]
                found[name] = v if dt == bf16 else v.bitcast(dt)
                found[name + " at"] = at
                at += k
            assert at <= tensor.shape[1], (at, tensor.shape)
            return found

        rows_s = sb("rows_s", [P, SLOTS * TG * PARTS * P], bf16)
        rows = rows_s[:, :].rearrange("p (s t n) -> p s t n", s=SLOTS, t=TG)
        gates_v = carve(rows_s, {f"g{i}": (CH, fp32) for i in range(5)})
        gr, gz, npre, cand, diff = (gates_v[f"g{i}"] for i in range(5))
        slo_f = carve(rows_s, {"v": (TQ * P, fp32)})["v"][0:QR, :]
        onehot_s = sb("onehot_s", [P, SLOTS * TG * P], bf16)
        onehot = onehot_s[:, :].rearrange("p (s n) -> p s n", s=SLOTS)
        onehot_slow = onehot_s[:, 0:TG * SWIN].rearrange("p (t n) -> p t n", n=SWIN)
        start_v = carve(onehot_s, {"pattern": (SWIN, i32), "zpad": (PARTS * P, bf16), "padrow": (2 * P, fp32),
                                   "tnext": (TQ, fp32)})
        pattern, zpad = start_v["pattern"], start_v["zpad"][0:BLOCKS * P - NODES, :]
        padrow, tnext = start_v["padrow"][0:1, :], start_v["tnext"][0:QR, :]
        win_s = sb("win_s", [P, P * BLOCKS], bf16)
        window = win_s[:, :].rearrange("p (b d) -> p b d", b=BLOCKS)
        win_bufs = [win_s[:, :], aggT[:, 0:P * BLOCKS // 2].bitcast(bf16)]
        reach = [aggT[:, 0:STRIPS], aggT[:, STRIPS:2 * STRIPS]]
        gathered = aggT[:, 2 * STRIPS:2 * STRIPS + UC * UT * 2 * P]
        win_v = carve(win_s, {"hs": (SLOTS * CH, fp32), "xn": (CJ * P, fp32), "lnT": (CH, fp32),
                              "rest": (CJ * P, fp32)})
        hs = win_v["hs"].rearrange("p (s n) -> p s n", s=SLOTS)
        xn, lnT, rest = win_v["xn"][0:CP, :], win_v["lnT"], win_v["rest"][0:CP, :]
        key_f = carve(win_s, {"v": (TQ * P, fp32)})["v"][0:QR, :]
        parts_s = sb("parts_s", [P, BLOCKS * PARTS * P], bf16)
        parts = parts_s[:, :].rearrange("p (b n) -> p b n", b=BLOCKS)
        wv = carve(parts_s, {"key": ((UNITS + PER) * UT, fp32), "slo": ((UNITS + PER) * UT, bf16), "lo_b": (GROUPS, fp32),
                             "iota_w": (SW, fp16), "kw": (2 * PER * UT, fp32), "sw": (2 * PER * UT, fp32),
                             "dist": (P, bf16), "setup": ((LAYERS + 3) * P, fp32),
                             "xrow": (SLOTS * CJ * P, fp32), "ol": (2 * 4 * UT * P, bf16),
                             "hrow": (SLOTS * CJ * PARTS * P, bf16), "oh": (OB * 2 * UT * SW, bf16)})
        keyT, sloT, lo_b, iota_w, kw, ol, oh = (wv[n] for n in ("key", "slo", "lo_b", "iota_w", "kw", "ol", "oh"))
        ohv = oh.rearrange("p (o t n) -> p o t n", o=OB, t=2 * UT)
        olv = ol.rearrange("p (o t n) -> p o t n", o=2, t=4 * UT)
        sw = wv["sw"].rearrange("p (o n) -> p o n", o=2)
        kw = kw.rearrange("p (o n) -> p o n", o=2)
        key_units = keyT[:, 0:UNITS * UT].rearrange("p (q i) -> p i q", i=UT)
        dist = wv["dist"]
        slo_units = sloT[:, 0:UNITS * UT].rearrange("p (q i) -> p i q", i=UT)
        found_v = carve(parts_s[:, wv["hrow at"]:], {n: (STRIPS, fp32) for n in ("delta", "code", "scratch")})
        delta, code, scratch = (found_v[n] for n in ("delta", "code", "scratch"))
        pattern_s, iota_r = delta.bitcast(i32), code.bitcast(fp16)[:, 0:STRIPS]
        below = scratch.bitcast(bf16).rearrange("p (o n) -> p o n", o=2)[0:QR, :, :]
        xrow = wv["xrow"][0:CP, :].rearrange("p (s n) -> p s n", s=SLOTS)
        hrow = wv["hrow"][0:CP, :].rearrange("p (s n) -> p s n", s=SLOTS)
        hrow_f = wv["hrow"][0:CP, :].bitcast(fp32).rearrange("p (s n) -> p s n", s=SLOTS)
        set_v = carve(wv["setup"].bitcast(bf16), {"wT": (LAYERS * P, fp32), "wih": (3 * P, fp32)})
        wT_sb, wih_sb = set_v["wT"].rearrange("p (l n) -> p l n", l=LAYERS), set_v["wih"]
        EW = TQ * P
        src_rows = aggT[0:QR, 0:EW].bitcast(i32)
        dst_rows = aggT[0:QR, EW:2 * EW].bitcast(i32)
        src_f = aggT[0:QR, EW:2 * EW]
        dst_f = aggT[0:QR, 2 * EW:3 * EW]
        rel_f = aggT[0:QR, 3 * EW:4 * EW]
        by_g = lambda a: a.rearrange("p (q g) -> p g q", g=TQ)

        def part_of(k, part):
            return hrow[:, k, :].rearrange("p (j n) -> p j n", j=CJ)[:, :, part * P:(part + 1) * P]

        sums = [ctx.enter_context(nc.psum_tensor(f"sums{i}", [P, 512], fp32)) for i in range(3)]
        pair = [ctx.enter_context(nc.psum_tensor(f"pair{i}", [P, 1024], fp32)) for i in range(2)]
        ps_misc = ctx.enter_context(nc.psum_tensor("ps_misc", [P, 512], fp32))
        ps_r, ps_z, ps_in = sums
        ps_hn, ps_rows = pair[0][:, 0:512], pair[0][:, 512:1024]
        ps_ln, ps_lin = pair[1][:, 0:512], pair[1][:, 512:1024]
        ps_dense = [b[:, 0:PARTS * P] for b in (pair[1], pair[1][:, 512:1024], pair[0])]
        ps_denseT = pair[0][:, 512:512 + P]
        banks4 = [pair[0][:, 0:512], pair[0][:, 512:1024], pair[1][:, 0:512], pair[1][:, 512:1024]]
        BANK = [0, 1, 2, 0, 1]

        s_src, s_dst, s_w = sem("src_loaded"), sem("dst_loaded"), sem("weights_loaded")
        s_const, s_iota = sem("constants_ready"), sem("iota_written")
        s_dve = sem("dve_setup_step")
        s_dstf, s_srcf, s_rel = sem("dst_as_float"), sem("src_as_float"), sem("rel_ready")
        s_slo, s_key = sem("slo_ready"), sem("key_ready")
        s_lo, s_lo_st, s_bases = sem("bases_int_ready"), sem("bases_stored"), sem("bases_loaded")
        s_min, s_min_st, s_next = sem("mins_ready"), sem("mins_stored"), sem("next_mins_loaded")
        s_cnt, s_cntP, s_strips = sem("below_counted"), sem("below_summed"), sem("strip_starts_ready")
        s_chk, s_chkP, s_wide = sem("checks_ready"), sem("checks_summed"), sem("wide_flag_ready")
        s_rows, s_uidx, s_ugot = sem("edge_rows_stored"), sem("unit_indices_ready"), sem("unit_tiles_gathered")
        s_ushift, s_uT, s_uC = sem("unit_keys_shifted"), sem("unit_lists_transposed"), sem("unit_lists_copied")
        s_relm, s_relP, s_relC = sem("placing_ready"), sem("columns_placed"), sem("columns_ready")
        s_kw, s_sw = sem("window_keys_ready"), sem("window_digits_ready")
        s_eT, s_eC = sem("edges_transposed"), sem("edges_copied")
        s_comb, s_combC = sem("combined_product"), sem("combined_copied")
        s_xload = sems("x_loaded")
        s_xused = sem("x_used")
        s_stats, s_var, s_std, s_xn = sem("ln_step"), sem("variance_ready"), sem("std_ready"), sem("x_normed")
        s_lnT, s_lnC, s_lin = sem("ln_transposed"), sem("ln_copied"), sem("linear_product")
        s_h0 = sem("state_written")
        s_kS = sems("state_stored")
        s_hload = sems("state_loaded")
        s_rT, s_hi, s_rest, s_mid, s_rC = (sem("rows_transposed"), sem("rows_hi"), sem("rows_rest"), sem("rows_mid"),
                                           sem("rows_staged"))
        s_rS = sems("rows_stored")
        s_pad = sem("table_padded")
        s_idx = sem("indices_ready")
        s_got = sems("rows_gathered")
        s_sum, s_taken, s_oh = sem("group_summed"), sem("sums_taken"), sem("onehot_ready")
        s_zero, s_agg = sem("agg_zeroed"), sem("layer_aggregated")
        s_sh, s_slow_oh = sem("slow_shifted"), sem("slow_onehot_ready")
        s_slow_sum, s_slow_add = sem("slow_window_summed"), sem("slow_window_added")
        s_dist, s_boa = sem("distances_ready"), sem("unit_src_onehot_by_scalar_ready")
        s_boh, s_bol, s_bsum, s_evac = (sem("unit_dst_onehot_ready"), sem("unit_src_onehot_ready"), sem("unit_pair_counted"),
                                        sem("unit_pair_copied"))
        s_aS, s_winfree = sem("window_stored"), sem("window_free")
        s_steer, s_lob = sem("steering_ready"), sem("lows_loaded")
        s_parts = sems("parts_loaded", PIECES)
        s_aL, s_used = sems("window_loaded", PIECES), sems("window_used", PIECES)
        s_dpart, s_dcopy, s_sel, s_dT, s_dadd = sem("dense_part_added"), sem("dense_copied"), sem("selection_ready"), sem("dense_transposed"), sem("dense_added")
        s_rz, s_n = sem("rz_product"), sem("n_product")
        s_rzread, s_nread = sem("gates_ready"), sem("n_pre_ready")
        s_t1, s_cand, s_d = sem("reset_applied"), sem("candidate_ready"), sem("update_step")
        s_passed = sem("wait_passed")

        def chunk_rows(t, c):
            return t[0:NODES, :].rearrange("(c p j) f -> p c (j f)", p=CP, j=CJ)[:, bass.ds(c, 1), :].rearrange(
                "p o n -> p (o n)")

        def wait_past(eng, semaphore, value):
            if isinstance(value, int) and value == 0:
                return
            eng.wait_ge(semaphore, value)

        def iterations(eng, count, body, peel):
            if peel:
                body(0)
            with eng.Fori(1 if peel else 0, count) as it:
                body(it)

        def steps(eng, count, step):
            for k in range(SLOTS):
                step(0, k, k == 0)
            with eng.Fori(1, count) as it:
                for k in range(SLOTS):
                    step(it, k, False)

        def norm_steps(eng, step):
            def iteration_of(it, last):
                for k in range(SLOTS):
                    following = (it, k + 1) if k < SLOTS - 1 else None if last else (it + 1, 0)
                    step(it, k, isinstance(it, int) and it == 0 and k == 0, following)
            iteration_of(0, False)
            with eng.Fori(1, CITER - 1) as it:
                iteration_of(it, False)
            iteration_of(CITER - 1, True)

        def load_skip(eng):
            eng.wait_ge(s_steer, 1)
            return (eng.value_load(skip_i[0:1, 0:1], min_val=0, max_val=GITER - DITER - 1),
                    eng.value_load(skip_i[0:1, 1:2], min_val=DITER + 1, max_val=GITER))

        def load_last(eng):
            return (eng.value_load(skip_i[0:1, 2:3], min_val=DITER, max_val=GITER - 1),
                    eng.value_load(skip_i[0:1, 3:4], min_val=0, max_val=GITER - DITER - 1))

        def iteration(skip, i):
            return nc.s_assert_within(skip + i, 0, GITER - 1,
                                      skip_runtime_bounds_check_because="i is below kept, and skip + kept is GITER")

        def dense_loops(eng, step):
            at_w = at_i = 0
            for loops, body, iters in RATES:
                rate = (body, iters, at_w, at_i)
                if at_w == 0:
                    step(0, rate)
                with eng.Fori(1 if at_w == 0 else 0, loops) as d:
                    step(d, rate)
                at_w, at_i = at_w + loops * body, at_i + loops * iters

        def block_range(s, rate):
            per = rate[0] * BLOCKS / (rate[1] * SLOTS)
            return [divmod(g, BLOCKS) for g in range(int(per * s + 0.001), int(per * (s + 1) + 0.001))]

        def window_steps(s, rate):
            return [("sum", a) if b == BLOCKS - 1 else ("add", a - 1) for a, b in block_range(s, rate)
                    if b in (BLOCKS - 1, LATER)]

        def dense_bank(a, rate):
            return ps_dense[a % (2 + rate[0] % 2)]

        def piece(b):
            return b * PIECES // BLOCKS

        with nc.Block() as block:

            @block.sync
            def _(sp):
                sp.dma_start(dst_rows, dst.rearrange("(q n) -> q n", q=QR)).then_inc(s_dst, 16)
                sp.dma_start(src_rows, src.rearrange("(q n) -> q n", q=QR)).then_inc(s_src, 16)
                sp.dma_start(wT_sb, weightT.rearrange("l k f -> k l f")).then_inc(s_w, 16)
                sp.dma_start(wih_sb, w_ihT).then_inc(s_w, 16)
                sp.dma_start(whh_sb[:, :], w_hhT).then_inc(s_w, 16)
                sp.dma_start(lin_sb[:, :], lin_wT).then_inc(s_w, 16)
                with nc.allow_non_contiguous_dma(reason="biases, one per partition"):
                    sp.dma_start(lin_bias[:, :], lin_b.rearrange("(p o) -> p o", o=1)).then_inc(s_w, 16)
                    sp.dma_start(bih[:, :], b_ih.rearrange("(g p) -> p g", p=P)).then_inc(s_w, 16)
                    sp.dma_start(bhh[:, :], b_hh.rearrange("(g p) -> p g", p=P)).then_inc(s_w, 16)
                sp.wait_ge(s_const, 11)
                sp.dma_start(table[NODES:BLOCKS * P, :], zpad).then_inc(s_pad, 16)
                sp.dma_start(edge_rows[TILES:TILES + 1, :], padrow).then_inc(s_rows, 16)
                sp.wait_ge(s_min, 1)
                sp.dma_start(mins_dram[0:QR, :], tmin[:, :]).then_inc(s_min_st, 16)
                sp.dma_start(mins_dram[QR:QR + 1, :], big[:, :]).then_inc(s_min_st, 16)
                sp.wait_ge(s_min_st, 32)
                sp.dma_start(tnext, mins_dram.rearrange("a b -> (a b)")[1:TILES + 1].rearrange(
                    "(q g) -> q g", g=TQ)).then_inc(s_next, 16)
                sp.wait_ge(s_lo, 1)
                sp.dma_start(bases_dram, lo_i[:, :]).then_inc(s_lo_st, 16)
                sp.dma_start(lows_dram, lo[:, :]).then_inc(s_lo_st, 16)
                sp.wait_ge(s_lo_st, 32)
                sp.dma_start(bases[:, :], bases_dram.rearrange("(o q) g -> o (q g)", o=1)).then_inc(s_bases, 16)
                sp.dma_start(lo_b, lows_dram.rearrange("(o q) g -> o (q g)", o=1).to_broadcast([P, GROUPS])).then_inc(s_lob, 16)
                by_tile = edge_rows[0:TILES, :].rearrange("(q g) n -> q g n", g=TQ)
                for i, (what, ready) in enumerate(((key_f, s_key), (slo_f, s_slo))):
                    sp.wait_ge(ready, 1)
                    sp.dma_start(by_tile[:, :, i * P:(i + 1) * P], what.rearrange("q (g n) -> q g n", n=P)).then_inc(s_rows, 16)

                def store_chunks(stage):
                    with sp.Fori(0, CITER) as it:
                        for k in range(SLOTS):
                            c = it * SLOTS + k
                            if stage < LAYERS:
                                sp.wait_ge(s_h0, c + (stage * CHUNKS + 1))
                                sp.dma_start(state[:, bass.ds(c * CH, CH)], hs[:, k, :]).then_inc(s_kS[k], 16)
                            sp.wait_ge(s_rC, c + (stage * CHUNKS + 1))
                            if stage < LAYERS:
                                sp.dma_start(chunk_rows(table, c), hrow[:, k, :]).then_inc(s_rS[k], 16)
                            else:
                                sp.dma_start(chunk_rows(out, c), hrow_f[:, k, 0:CJ * P]).then_inc(s_rS[k], 16)

                store_chunks(0)
                sp.wait_ge(s_wide, 1)
                wide = sp.value_load(wide_i[0:1, 0:1], min_val=0, max_val=1)
                sp.wait_ge(s_pad, 16)
                with sp.Fori(0, DWINS // 2) as i:
                    for o in range(2):
                        w = i * 2 + o
                        sp.wait_ge(s_evac, w * PAIRS + (PAIRS + 2))
                        sp.dma_start(counts[bass.ds(w, 1), :, :].rearrange("w p n -> p (w n)"),
                                     win_bufs[o]).then_inc(s_aS, 16)
                        sp.wait_ge(s_aS, w * 16 + 16)
                        sp.sem_inc(s_winfree, 1)

                def load_window(layer, j, with_parts=False):
                    w = j + layer * DWINS
                    for h in range(PIECES):
                        b = [b for b in range(BLOCKS) if piece(b) == h]
                        n = slice(b[0] * P, (b[-1] + 1) * P)
                        if with_parts:
                            sp.dma_start(parts[:, b[0]:b[-1] + 1, :],
                                         table.rearrange("(b p) n -> p b n", p=P)[:, b[0]:b[-1] + 1, :]).then_inc(
                                s_parts[h], 16)
                        wait_past(sp, s_used[h], w)
                        sp.dma_start(win_s[:, n], counts[bass.ds(j, 1), :, n].rearrange("w p n -> p (w n)")).then_inc(
                            s_aL[h], 16)

                for stage in range(1, LAYERS + 1):
                    for k in range(SLOTS):
                        sp.wait_ge(s_rS[k], 16 * CITER * stage)
                        sp.wait_ge(s_kS[k], 16 * CITER * stage)
                    with sp.If(wide):
                        sp.sem_inc(s_passed, 1)
                    with sp.Else():
                        sp.wait_ge(s_aS, 16 * DWINS)
                        sp.wait_ge(s_boa, (DWINS + 1) * (PAIRS // 2) + 2)
                        load_window(stage - 1, 0, with_parts=True)
                        with sp.Fori(1, DWINS) as j:
                            load_window(stage - 1, j)
                    store_chunks(stage)
                for k in range(SLOTS):
                    sp.wait_ge(s_rS[k], 16 * CITER * (LAYERS + 1))
                    sp.wait_ge(s_kS[k], 16 * CITER * LAYERS)

            @block.gpsimd
            def _(pool):
                nc.gpsimd.memset(ident[:, :], 0.0).then_inc(s_iota, 1)
                nc.gpsimd.iota(pattern, pattern=[[1, SWIN]], base=0, channel_multiplier=0).then_inc(s_iota, 1)
                nc.gpsimd.memset(eps_t[:, :], EPS).then_inc(s_const, 1)
                nc.gpsimd.memset(ones[:, :], 1.0).then_inc(s_const, 1)
                nc.gpsimd.memset(zpad, 0.0).then_inc(s_const, 1)
                nc.gpsimd.memset(padrow, -1.0).then_inc(s_const, 1)
                nc.gpsimd.memset(big[:, :], 1.0e9).then_inc(s_const, 1)
                pool.wait_ge(s_iota, 2)
                nc.gpsimd.tensor_copy(iota_w, pattern[:, 0:SW]).then_inc(s_iota, 1)
                nc.gpsimd.tensor_copy(iota_b[:, :], pattern[:, 0:WIN]).then_inc(s_iota, 1)
                nc.gpsimd.tensor_copy(iota_s[:, :], pattern[:, 0:SWIN]).then_inc(s_iota, 1)
                nc.gpsimd.affine_select(out=ident[:, :], in_=ident[:, :], compare_op=ALU.not_equal, fill=1.0, base=0,
                                        pattern=[[-1, P]], channel_multiplier=1).then_inc(s_const, 1)
                pool.wait_ge(s_iota, 5)
                nc.gpsimd.iota(pattern_s, pattern=[[1, STRIPS]], base=0, channel_multiplier=0).then_inc(s_iota, 1)
                pool.wait_ge(s_iota, 6)
                nc.gpsimd.tensor_copy(iota_r, pattern_s).then_inc(s_const, 1)
                nc.gpsimd.iota(ulist_i[:, :], pattern=[[P, UC]], base=0, channel_multiplier=1).then_inc(s_iota, 1)
                pool.wait_ge(s_iota, 7)
                nc.gpsimd.tensor_copy(unit_no, ulist_i[:, :]).then_inc(s_const, 1)
                nc.gpsimd.memset(one[:, :], 1.0).then_inc(s_const, 1)
                nc.gpsimd.memset(sloT[:, UNITS * UT:], 0.0).then_inc(s_const, 1)
                nc.gpsimd.memset(keyT[:, UNITS * UT:], 0.0).then_inc(s_const, 1)

                def load_x(uses):
                    with pool.Fori(0, CITER) as it:
                        for k in range(SLOTS):
                            c = it * SLOTS + k
                            pool.wait_ge(s_xused, c + uses * CHUNKS + 1)
                            pool.dma_start(xrow[:, k, :], chunk_rows(x, c)).then_inc(s_xload[k], 16)
                            if uses:
                                load_state(LAYERS - 1, it, k)

                def load_state(layer, it, k):
                    c = it * SLOTS + k
                    if layer < LAYERS - 1:
                        pool.wait_ge(s_kS[k], (it + (layer + 1) * CITER) * 16)
                    else:
                        pool.wait_ge(s_kS[k], 16 * CITER * LAYERS)
                    pool.wait_ge(s_rT, c + ((layer + 1) * CHUNKS - SLOTS + 1))
                    pool.dma_start(hs[:, k, :], state[:, bass.ds(c * CH, CH)]).then_inc(s_hload[k], 16)

                pool.wait_ge(s_rows, 48)
                pool.wait_ge(s_uidx, 1)
                pool.sem_inc(s_passed, 1)
                for c in range(UC):
                    for i in range(UT):
                        at = (c * UT + i) * 2 * P
                        pool.indirect_dma_start(gathered[:, at:at + 2 * P], None, edge_rows,
                                                bass.IndirectOffsetOnAxis(ap=unit_idx[:, c, i:i + 1], axis=0)).then_inc(s_ugot, 16)
                load_x(0)
                pool.wait_ge(s_uC, 2 * UC)
                pool.sem_inc(s_passed, 1)
                with pool.Fori(0, DWINS // 2) as i:
                    for o in range(2):
                        w = i * 2 + o
                        pool.wait_ge(s_sw, w + 1)
                        pool.sem_inc(s_passed, 1)
                        for m in range(PAIRS // 2):
                            b = w * PAIRS + m * 2
                            pool.wait_ge(s_bsum, b + 2)
                            pool.sem_inc(s_passed, 1)
                            for t in range(ON_SCALAR + 1, 4 * UT):
                                ins = nc.gpsimd.tensor_scalar(olv[:, m % 2, t, :], iota_b[:, :],
                                                              sw[:, o, m * 4 * UT + t:m * 4 * UT + t + 1], None, ALU.is_equal)
                            ins.then_inc(s_bol, 1)
                skip, kept = load_skip(pool)
                for layer in range(LAYERS):
                    for k in range(SLOTS):
                        pool.wait_ge(s_rS[k], 16 * CITER * (layer + 1))
                    with pool.Fori(0, kept) as i:
                        u = i + kept * layer if layer else i
                        for k in range(SLOTS):
                            n = u * SLOTS + k
                            pool.wait_ge(s_idx, n + 1)
                            pool.wait_ge(s_sum, n + 1)
                            pool.sem_inc(s_passed, 1)
                            for j in range(TG):
                                pool.indirect_dma_start(
                                    rows[:, k, j, :], None, table,
                                    bass.IndirectOffsetOnAxis(ap=idx[:, k, j:j + 1], axis=0)).then_inc(s_got[k], 16)
                    pool.wait_ge(s_agg, layer + 1)
                    if layer < LAYERS - 1:
                        with pool.Fori(0, CITER) as it:
                            for k in range(SLOTS):
                                load_state(layer, it, k)
                    else:
                        load_x(1)

            @block.tensor
            def _(pe):
                pe.sem_inc(s_sum, SLOTS)
                pe.sem_inc(s_bsum, OB)
                pe.wait_ge(s_const, 11)

                n = 0
                for what, ready in ((dst_f, s_dstf), (rel_f, s_rel), (src_f, s_srcf)):
                    pe.wait_ge(ready, 1)
                    for g in range(TQ):
                        if n >= 2:
                            pe.wait_ge(s_eC, n - 1)
                        nc.tensor.transpose(sums[n % 2][:, 0:QR], what[:, g * P:(g + 1) * P],
                                            ident[0:QR, 0:QR]).then_inc(s_eT, 1)
                        n += 1
                pe.wait_ge(s_chk, 1)
                nc.tensor.matmul(ps_misc[:, 0:2], ones[0:QR, :], faults[:, :], start=True, stop=True).then_inc(s_chkP, 1)
                w = STRIPS // SPL
                for g in range(TQ):
                    pe.wait_ge(s_cnt, g + 1)
                    for i in range(SPL):
                        t = nc.tensor.matmul(banks4[i][:, 0:w], ones[0:QR, :], below[:, g % 2, i * w:(i + 1) * w],
                                             start=(g == 0), stop=(g == TQ - 1))
                    t.then_inc(s_cntP, 1)

                pe.wait_ge(s_w, 16 * 7)
                pe.wait_ge(s_eC, n)
                for layer in range(LAYERS):
                    nc.tensor.matmul(sums[layer][:, 0:3 * P], wT_sb[:, layer, :], wih_sb, start=True,
                                     stop=True).then_inc(s_comb, 1)
                pe.wait_ge(s_strips, 1)
                for k in range(P // PER):
                    pe.wait_ge(s_relm, k + 1)
                    nc.tensor.matmul(ps_misc[:, k * UC:(k + 1) * UC], select[:, :], unit_strip, start=True, stop=True)
                    nc.tensor.matmul(ps_misc[0:1, (4 + k) * UC:(5 + k) * UC], ident[:, k * PER:k * PER + 1], unit_strip,
                                     start=True, stop=True).then_inc(s_relP, 1)
                pe.wait_ge(s_combC, 1)
                pe.wait_ge(s_ushift, 1)
                for c in range(UC):
                    if c >= 2:
                        pe.wait_ge(s_uC, 2 * c - 2)
                    for half in range(2):
                        for i in range(UT):
                            at = (c * UT + i) * 2 * P + half * P
                            t = nc.tensor.transpose(sums[c % 2][:, (half * UT + i) * P:(half * UT + i + 1) * P],
                                                    gathered[:, at:at + P], ident[:, :])
                    t.then_inc(s_uT, 1)

                def transpose_rows(k, u):
                    pe.wait_ge(s_h0, u + 1)
                    wait_past(pe, s_rest, u)
                    for j in range(CJ):
                        t = nc.tensor.transpose(ps_rows[0:CP, j * P:(j + 1) * P], hs[:, k, bass.ds(j, CP, CJ)],
                                                ident[:, :])
                    t.then_inc(s_rT, 1)

                def linear_step(it, k, first):
                    c = it * SLOTS + k
                    pe.wait_ge(s_xn, c + 1)
                    wait_past(pe, s_lnC, c)
                    for j in range(CJ):
                        t = nc.tensor.transpose(ps_ln[:, j * CP:(j + 1) * CP], xn[:, j * P:(j + 1) * P],
                                                ident[0:CP, 0:CP])
                    t.then_inc(s_lnT, 1)
                    if not first:
                        transpose_rows((k - 1) % SLOTS, c - 1)
                    pe.wait_ge(s_lnC, c + 1)
                    wait_past(pe, s_h0, c)
                    nc.tensor.matmul(ps_lin[:, 0:CH], lin_sb[:, :], lnT, start=True, stop=True).then_inc(s_lin, 1)

                steps(pe, CITER, linear_step)
                transpose_rows(SLOTS - 1, CHUNKS - 1)
                pe.wait_ge(s_wide, 1)
                wide = pe.value_load(wide_i[0:1, 0:1], min_val=0, max_val=1)

                def group_product(u, k):
                    n = u * SLOTS + k
                    pe.wait_ge(s_oh, n + 1)
                    pe.wait_ge(s_taken, n + 1)
                    pe.wait_ge(s_got[k], (u + 1) * (16 * TG))
                    for j in range(TG):
                        for part in range(PARTS):
                            t = nc.tensor.matmul(sums[BANK[k]][:, 0:WIN], rows[:, k, j, part * P:(part + 1) * P],
                                                 onehot[:, k, j * P:(j + 1) * P], start=(j == 0 and part == 0),
                                                 stop=(j == TG - 1 and part == PARTS - 1))
                    t.then_inc(s_sum, 1)

                def build_window(w):
                    for m in range(PAIRS):
                        b = w * PAIRS + m
                        pe.wait_ge(s_evac, b + 1)
                        pe.wait_ge(s_boh, b + 2)
                        if m % 2 == 0:
                            pe.wait_ge(s_bol, w * (PAIRS // 2) + (m // 2 + 1 + PAIRS))
                            pe.wait_ge(s_boa, w * (PAIRS // 2) + (m // 2 + 1 + PAIRS // 2))
                        for j in range(2):
                            for i in range(UT):
                                t = nc.tensor.matmul(pair[m % 2][:, j * 512:j * 512 + SW],
                                                     olv[:, m // 2 % 2, (m % 2 * 2 + j) * UT + i, :],
                                                     ohv[:, m % OB, j * UT + i, :], start=(i == 0), stop=(i == UT - 1))
                        t.then_inc(s_bsum, 1)

                def dense_block(w, bank, b):
                    if b == 0:
                        wait_past(pe, s_dcopy, max(w - 1, 0) if isinstance(w, int) else w - 1)
                    if b == 0 or piece(b) != piece(b - 1):
                        pe.wait_ge(s_aL[piece(b)], (w + 1) * 16)
                        if isinstance(w, int):
                            pe.wait_ge(s_parts[piece(b)], (w // DWINS + 1) * 16)
                    t = nc.tensor.matmul(bank, window[:, b, :], parts[:, b, :], start=(b == 0),
                                         stop=(b == BLOCKS - 1))
                    if b == BLOCKS - 1 or piece(b) != piece(b + 1):
                        t.then_inc(s_used[piece(b)], 1)

                def dense_transpose(w):
                    pe.wait_ge(s_sel, w + 1)
                    pe.wait_ge(s_dcopy, w + 1)
                    wait_past(pe, s_dadd, w)
                    nc.tensor.matmul(ps_denseT, dsum[:, :], select[:, :], start=True, stop=True).then_inc(s_dT, 1)

                def slow_groups(layer):
                    with pe.Fori(0, GITER) as it:
                        for k in range(SLOTS):
                            n = it * SLOTS + (k + layer * GROUPS)
                            pe.wait_ge(s_got[k], (it + (layer * GITER + 1)) * (16 * TG))
                            pe.sem_inc(s_passed, 1)
                            with pe.Fori(0, SWINS) as w:
                                pe.wait_ge(s_slow_oh, n * SWINS + w + 1)
                                for j in range(TG):
                                    for part in range(PARTS):
                                        t = nc.tensor.matmul(sums[0][:, 0:SWIN], rows[:, k, j, part * P:(part + 1) * P],
                                                             onehot_slow[:, j, :], start=(j == 0 and part == 0),
                                                             stop=(j == TG - 1 and part == PARTS - 1))
                                t.then_inc(s_slow_sum, 1)
                            pe.wait_ge(s_slow_sum, (n + 1) * SWINS)
                            pe.sem_inc(s_sum, 1)

                with pe.Fori(0, DWINS) as w:
                    build_window(w)
                skip, kept = load_skip(pe)
                for layer in range(LAYERS):
                    with pe.If(wide):
                        slow_groups(layer)
                    with pe.Else():
                        past = kept * layer if layer else 0

                        def dense_step(d, rate):
                            body, iters, at_w, at_i = rate
                            for s in range(iters * SLOTS):
                                group_product(past + d * iters + (at_i + s // SLOTS), s % SLOTS)
                                for a, b in block_range(s, rate):
                                    w = d * body + (at_w + a + layer * DWINS)
                                    dense_block(w, dense_bank(a, rate), b)
                                    if b == LATER and not (isinstance(d, int) and a == 0):
                                        dense_transpose(w - 1)

                        dense_loops(pe, dense_step)
                        dense_transpose(layer * DWINS + (DWINS - 1))
                        with pe.Fori(DITER, kept) as i:
                            for k in range(SLOTS):
                                group_product(past + i, k)

                    pe.wait_ge(s_agg, layer + 1)

                    def gates(it, k):
                        c = it * SLOTS + k
                        v = c + layer * CHUNKS
                        h = hs[:, k, :]
                        a = aggT[:, bass.ds(c * CH, CH)]
                        pe.wait_ge(s_hload[k], (it + (layer * CITER + 1)) * 16)
                        wait_past(pe, s_rzread, v)
                        for g, ps in ((0, ps_r), (1, ps_z)):
                            nc.tensor.matmul(ps[:, 0:CH], comb[:, layer, g * P:(g + 1) * P], a, start=True, stop=False)
                            t = nc.tensor.matmul(ps[:, 0:CH], whh_sb[:, g * P:(g + 1) * P], h, start=False, stop=True)
                        t.then_inc(s_rz, 1)
                        wait_past(pe, s_nread, v)
                        nc.tensor.matmul(ps_in[:, 0:CH], comb[:, layer, 2 * P:3 * P], a, start=True, stop=True)
                        nc.tensor.matmul(ps_hn[:, 0:CH], whh_sb[:, 2 * P:3 * P], h, start=True,
                                         stop=True).then_inc(s_n, 1)

                    def step(it, k, first):
                        gates(it, k)
                        if not first:
                            transpose_rows((k - 1) % SLOTS, it * SLOTS + (k + (layer + 1) * CHUNKS - 1))

                    steps(pe, CITER, step)
                    transpose_rows(SLOTS - 1, (layer + 2) * CHUNKS - 1)

            @block.scalar
            def _(act):
                n = 0
                for to in (dstT[:, :], relT[:, :], srcT[:, :]):
                    for g in range(TQ):
                        act.wait_ge(s_eT, n + 1)
                        nc.scalar.copy(by_g(to)[:, g, :], sums[n % 2][:, 0:QR]).then_inc(s_eC, 1)
                        n += 1
                for layer in range(LAYERS):
                    act.wait_ge(s_comb, layer + 1)
                    t = nc.scalar.copy(comb[:, layer, :], sums[layer][:, 0:3 * P])
                t.then_inc(s_combC, 1)
                for c in range(UC):
                    act.wait_ge(s_uT, c + 1)
                    for half, to in enumerate((key_units, slo_units)):
                        nc.scalar.copy(to[:, :, c * P:(c + 1) * P],
                                       sums[c % 2][:, half * UT * P:(half + 1) * UT * P].rearrange("p (i q) -> p i q", i=UT)
                                       ).then_inc(s_uC, 1)

                def rows_hi(it, k, u, stage):
                    act.wait_ge(s_rT, u + 1)
                    wait_past(act, s_rS[k], (it + stage * CITER) * 16)
                    nc.scalar.copy(part_of(k, 0), ps_rows[0:CP, :].rearrange("p (j n) -> p j n", j=CJ)).then_inc(s_hi, 1)

                def rows_mid(k, u):
                    act.wait_ge(s_rest, u + 1)
                    nc.scalar.copy(part_of(k, 1), rest.rearrange("p (j n) -> p j n", j=CJ)).then_inc(s_mid, 1)

                def deviation(it, k):
                    act.wait_ge(s_var, it * SLOTS + k + 1)
                    nc.scalar.activation(rstd[:, :], mv[:, :, 1], ACT.Sqrt, bias=eps_t[0:CP, :]).then_inc(s_std, 1)

                def linear_step(it, k, first, following):
                    c = it * SLOTS + k
                    before = (k - 1) % SLOTS
                    if first:
                        deviation(0, 0)
                    act.wait_ge(s_lnT, c + 1)
                    wait_past(act, s_lin, c)
                    nc.scalar.activation(lnT.rearrange("f (p j) -> f j p", j=CJ),
                                         ps_ln[:, 0:CH].rearrange("f (j p) -> f j p", j=CJ), ACT.Relu).then_inc(s_lnC, 1)
                    if following:
                        deviation(*following)
                    if not first:
                        rows_hi(it - (k == 0) if k else it - 1, before, c - 1, 0)
                        rows_mid(before, c - 1)
                    act.wait_ge(s_lin, c + 1)
                    wait_past(act, s_kS[k], it * 16)
                    if not (isinstance(it, int) and it == 0):
                        act.wait_ge(s_rT, c - SLOTS + 1)
                    nc.scalar.activation(hs[:, k, :], ps_lin[:, 0:CH], ACT.Identity, bias=lin_bias[:, :]).then_inc(s_h0, 1)

                norm_steps(act, linear_step)
                rows_hi(CITER - 1, SLOTS - 1, CHUNKS - 1, 0)
                rows_mid(SLOTS - 1, CHUNKS - 1)
                act.wait_ge(s_wide, 1)
                wide = act.value_load(wide_i[0:1, 0:1], min_val=0, max_val=1)

                def hand_indices(it, u, k):
                    wait_past(act, s_got[k], u * (16 * TG))
                    nc.scalar.copy(idx[:, k, :], srcT[:, bass.ds((it * SLOTS + k) * TG, TG)]).then_inc(s_idx, 1)

                act.wait_ge(s_strips, 1)
                for k in range(SLOTS):
                    act.wait_ge(s_kS[k], 16 * CITER)
                act.sem_inc(s_winfree, 2)
                act.sem_inc(s_evac, 2)
                def src_onehot(o, n, w):
                    at = n * 4 * UT + ON_SCALAR
                    act.wait_ge(s_boa, w * (PAIRS // 2) + (n + PAIRS // 2))
                    nc.scalar.activation(dist, iota_b[:, :], ACT.Abs, bias=sw[:, o, at:at + 1], scale=-1.0).then_inc(s_dist, 1)
                    act.wait_ge(s_dist, w * (PAIRS // 2) + (n + 1))
                    nc.scalar.activation(olv[:, n % 2, ON_SCALAR, :], dist, ACT.Relu, bias=one[:, :],
                                         scale=-1.0).then_inc(s_boa, 1)

                act.wait_ge(s_const, 11)
                act.wait_ge(s_sw, 1)
                for n in range(2):
                    src_onehot(0, n, 0)
                with act.Fori(0, DWINS // 2) as i:
                    for o in range(2):
                        w = i * 2 + o
                        act.wait_ge(s_winfree, w + 1)
                        to = win_bufs[o].rearrange("p (b d) -> p d b", b=BLOCKS)
                        for m in range(PAIRS):
                            act.wait_ge(s_bsum, w * PAIRS + (m + OB + 1))
                            nc.scalar.copy(to[:, m * 2 * SUB:(m + 1) * 2 * SUB, :].rearrange("p (u d) b -> p u d b", u=2),
                                           pair[m % 2][:, :].rearrange("p (u n) -> p u n", u=2)[:, :, 0:SW].rearrange(
                                               "p u (d b) -> p u d b", b=BLOCKS)).then_inc(s_evac, 1)
                            n = m // 2 + 2
                            if m % 2 and n < PAIRS // 2:
                                src_onehot(o, n, w)
                            elif m % 2:
                                act.wait_ge(s_sw, w + 2)
                                src_onehot(1 - o, n - PAIRS // 2, w + 1)

                skip, kept = load_skip(act)
                last, more = load_last(act)
                for layer in range(LAYERS):
                    past = kept * layer if layer else 0

                    def hand(i, k):
                        hand_indices(iteration(skip, i), past + i, k)

                    def hand_ahead(i, k):
                        k += AHEAD
                        hand(i + k // SLOTS, k % SLOTS)

                    with act.If(wide):
                        iterations(act, GITER, lambda i: [hand(i, k) for k in range(SLOTS)], peel=True)
                    with act.Else():
                        for k in range(AHEAD):
                            hand(0, k)

                        def dense_step(d, rate):
                            _, iters, _, at_i = rate
                            for s in range(iters * SLOTS):
                                hand_ahead(d * iters + (at_i + s // SLOTS), s % SLOTS)

                        dense_loops(act, dense_step)
                        with act.If(more):
                            with act.Fori(DITER, last) as i:
                                for k in range(SLOTS):
                                    hand_ahead(i, k)
                        for k in range(AHEAD, SLOTS):
                            hand(last, k)

                    def step(it, k, first):
                        c = it * SLOTS + k
                        v = c + layer * CHUNKS
                        before = (k - 1) % SLOTS
                        publish = not first and layer < LAYERS - 1
                        act.wait_ge(s_rz, v + 1)
                        act.wait_ge(s_h0, v + CHUNKS)
                        nc.scalar.activation(gr, ps_r[:, 0:CH], ACT.Sigmoid, bias=brz[:, 0:1])
                        nc.scalar.activation(gz, ps_z[:, 0:CH], ACT.Sigmoid, bias=brz[:, 1:2]).then_inc(s_rzread, 1)
                        if publish:
                            rows_hi(it - (k == 0), before, v + (CHUNKS - 1), layer + 1)
                        act.wait_ge(s_nread, v + 1)
                        nc.scalar.activation(cand, npre, ACT.Tanh, bias=bih[:, 2:3]).then_inc(s_cand, 1)
                        if publish:
                            rows_mid(before, v + (CHUNKS - 1))

                    steps(act, CITER, step)
                    if layer < LAYERS - 1:
                        rows_hi(CITER - 1, SLOTS - 1, (layer + 2) * CHUNKS - 1, layer + 1)
                        rows_mid(SLOTS - 1, (layer + 2) * CHUNKS - 1)

            @block.vector
            def _(dve):
                done = [0]

                def then(ins):
                    done[0] += 1
                    ins.then_inc(s_dve, 1)
                    dve.wait_ge(s_dve, done[0])

                dve.sem_inc(s_taken, 2)
                dve.sem_inc(s_xused, SLOTS)
                dve.wait_ge(s_dst, 16)
                nc.vector.tensor_copy(dst_f, dst_rows).then_inc(s_dstf, 1)
                dve.wait_ge(s_dstf, 1)
                tiled = dst_f.rearrange("q (g n) -> q g n", n=P)
                nc.vector.tensor_reduce(tmin[:, :], tiled, AX.X, ALU.min).then_inc(s_min, 1)
                then(nc.vector.tensor_reduce(tmax[:, :], tiled, AX.X, ALU.max))
                dve.wait_ge(s_min, 1)
                then(nc.vector.tensor_reduce(lo[:, :], tmin[:, :].rearrange("q (g t) -> q g t", t=TG), AX.X, ALU.min))
                then(nc.vector.tensor_reduce(hi[:, :], tmax[:, :].rearrange("q (g t) -> q g t", t=TG), AX.X, ALU.max))
                nc.vector.tensor_copy(lo_i[:, :], lo[:, :]).then_inc(s_lo, 1)
                nc.vector.tensor_tensor(rel_f.rearrange("q (g n) -> q g n", n=TG * P),
                                        dst_f.rearrange("q (g n) -> q g n", n=TG * P),
                                        lo[:, :].unsqueeze(2).broadcast_to([QR, GQ, TG * P]),
                                        ALU.subtract).then_inc(s_rel, 1)
                then(nc.vector.tensor_tensor(hi[:, :], hi[:, :], lo[:, :], ALU.subtract))
                then(nc.vector.tensor_reduce(checks[:, 0:1], hi[:, :], AX.X, ALU.max))
                dve.wait_ge(s_src, 16)
                nc.vector.tensor_copy(src_f, src_rows).then_inc(s_srcf, 1)
                then(nc.vector.tensor_scalar(key_f.bitcast(i32), src_rows, 7, None, ALU.arith_shift_right))
                then(nc.vector.tensor_copy(slo_f, key_f.bitcast(i32)))
                nc.vector.scalar_tensor_tensor(out=key_f, in0=dst_f, scalar=float(BLOCKS), in1=slo_f, op0=ALU.mult,
                                               op1=ALU.add).then_inc(s_key, 1)
                dve.wait_ge(s_key, 1)
                dve.wait_ge(s_srcf, 1)
                nc.vector.scalar_tensor_tensor(out=slo_f, in0=slo_f, scalar=-float(P), in1=src_f, op0=ALU.mult,
                                               op1=ALU.add).then_inc(s_slo, 1)
                dve.wait_ge(s_next, 16)
                then(nc.vector.tensor_tensor(tnext, tmax[:, :], tnext, ALU.is_gt))
                then(nc.vector.tensor_reduce(checks[:, 1:2], tnext, AX.X, ALU.max))
                then(nc.vector.tensor_copy(faults[:, 1:2], checks[:, 1:2]))
                nc.vector.tensor_scalar(faults[:, 0:1], checks[:, 0:1], float(WIN), None, ALU.is_ge).then_inc(s_chk, 1)
                dve.wait_ge(s_const, 11)
                then(nc.vector.tensor_copy(tmin_i[:, :], tmin[:, :]))
                then(nc.vector.tensor_scalar(tmin_i[:, :], tmin_i[:, :], SUB.bit_length() - 1, None, ALU.arith_shift_right))
                then(nc.vector.tensor_copy(tstrip[:, :], tmin_i[:, :]))
                for g in range(TQ):
                    if g >= 2:
                        dve.wait_ge(s_cntP, g - 1)
                    nc.vector.tensor_scalar(below[:, g % 2, :], iota_r[0:QR, :], tstrip[:, g:g + 1], None,
                                            ALU.is_ge).then_inc(s_cnt, 1)
                dve.wait_ge(s_chkP, 1)
                nc.vector.tensor_scalar(wide_i[:, :], ps_misc[0:1, 0:1], 0.0, None, ALU.is_gt).then_inc(s_wide, 1)
                then(nc.vector.tensor_reduce(ok_b, ps_misc[:, 0:2], AX.X, ALU.max))
                then(nc.vector.tensor_scalar(ok_b, ok_b, 0.0, None, ALU.is_le))
                dve.wait_ge(s_cntP, TQ)
                dve.wait_ge(s_eC, 3 * TQ)
                starts, units_of = reach
                w = STRIPS // SPL
                for i in range(SPL):
                    t = nc.vector.tensor_scalar(starts[:, i * w:(i + 1) * w], banks4[i][:, 0:w], 1.0, None, ALU.max)
                    t.then_inc(s_strips if i == SPL - 1 else s_dve, 1)
                done[0] += SPL - 1
                dve.wait_ge(s_strips, 1)
                dve.wait_ge(s_dve, done[0])
                then(nc.vector.tensor_scalar(delta[:, 0:1], starts[:, 0:1], 1.0, None, ALU.subtract))
                then(nc.vector.tensor_tensor(delta[:, 1:STRIPS], starts[:, 1:STRIPS], starts[:, 0:STRIPS - 1], ALU.subtract))
                whole = scratch.bitcast(i32)
                then(nc.vector.tensor_scalar(whole, delta, 2.0, None, ALU.add))
                then(nc.vector.tensor_scalar(whole, whole, 1, None, ALU.arith_shift_right))
                then(nc.vector.tensor_copy(units_of, whole))
                then(nc.vector.scalar_tensor_tensor(out=code, in0=units_of, scalar=-float(UT), in1=delta, op0=ALU.mult,
                                                    op1=ALU.add))
                then(nc.vector.tensor_scalar(code, code, float(BIG), None, ALU.add))
                now, reach_by, n = 1, 1, STRIPS
                while reach_by < n:
                    a, b = reach[now], reach[1 - now]
                    then(nc.vector.tensor_copy(b[:, 0:reach_by], a[:, 0:reach_by]))
                    then(nc.vector.tensor_tensor(b[:, reach_by:n], a[:, reach_by:n], a[:, 0:n - reach_by], ALU.add))
                    now, reach_by = 1 - now, reach_by * 2
                upto = reach[now]
                for c in range(UC):
                    then(nc.vector.scalar_tensor_tensor(out=scratch, in0=upto, scalar=unit_no[:, c:c + 1], in1=code,
                                                        op0=ALU.is_le, op1=ALU.mult))
                    then(nc.vector.tensor_reduce(unit_sum[:, c:c + 1], scratch, AX.X, ALU.add))
                then(nc.vector.tensor_scalar(scratch, upto, float(UNITS), None, ALU.is_le))
                then(nc.vector.tensor_reduce(reached, scratch, AX.X, ALU.add))
                then(nc.vector.scalar_tensor_tensor(out=scratch, in0=upto, scalar=float(UNITS), in1=delta,
                                                    op0=ALU.is_le, op1=ALU.mult))
                then(nc.vector.tensor_reduce(spared, scratch, AX.X, ALU.add))
                then(nc.vector.tensor_scalar(ulist_i[:, :], unit_sum, float(BIG - 1), None, ALU.add))
                then(nc.vector.tensor_scalar(ulist_i[:, :], ulist_i[:, :], BIG.bit_length() - 1, None,
                                             ALU.arith_shift_right))
                then(nc.vector.tensor_copy(unit_strip, ulist_i[:, :]))
                then(nc.vector.scalar_tensor_tensor(out=unit_tile, in0=unit_strip, scalar=-float(BIG), in1=unit_sum,
                                                    op0=ALU.mult, op1=ALU.add))
                then(nc.vector.scalar_tensor_tensor(out=unit_tile, in0=unit_no, scalar=float(UT), in1=unit_tile,
                                                    op0=ALU.mult, op1=ALU.add))
                then(nc.vector.tensor_scalar(unit_live, unit_strip, reached, ok_b, ALU.is_lt, ALU.mult))
                for i in range(UT):
                    then(nc.vector.tensor_scalar(unit_sum, unit_tile, float(TILES - i), None, ALU.subtract))
                    then(nc.vector.tensor_tensor(unit_sum, unit_sum, unit_live, ALU.mult))
                    then(nc.vector.tensor_scalar(unit_idx[:, :, i], unit_sum, float(TILES), None, ALU.add))
                    then(nc.vector.tensor_scalar(unit_shift[:, :, i], unit_strip, float(SW), None, ALU.mult))
                dve.sem_inc(s_uidx, 1)
                then(nc.vector.tensor_scalar(limit_b, reached, float(SUB), ok_b, ALU.mult, ALU.mult))
                then(nc.vector.tensor_scalar(spared, spared, 5243.0, None, ALU.mult))
                then(nc.vector.tensor_copy(skip_i[:, 0:1], spared[0:1, :]))
                then(nc.vector.tensor_scalar(skip_i[:, 0:1], skip_i[:, 0:1], 17, None, ALU.arith_shift_right))
                then(nc.vector.tensor_copy(spared[0:1, :], skip_i[:, 0:1]))
                then(nc.vector.tensor_scalar(spared[0:1, :], spared[0:1, :], float(GITER - DITER - 1), ok_b[0:1, :],
                                             ALU.min, ALU.mult))
                then(nc.vector.tensor_copy(skip_i[:, 0:1], spared[0:1, :]))
                then(nc.vector.tensor_scalar(skip_i[:, 3:4], spared[0:1, :], -1.0, float(GITER - DITER - 1), ALU.mult, ALU.add))
                then(nc.vector.tensor_scalar(skip_i[:, 2:3], spared[0:1, :], -1.0, float(GITER - 1), ALU.mult, ALU.add))
                nc.vector.tensor_scalar(skip_i[:, 1:2], spared[0:1, :], -1.0, float(GITER), ALU.mult,
                                        ALU.add).then_inc(s_steer, 1)
                dve.wait_ge(s_bases, 16)
                then(nc.vector.tensor_scalar(bases[:, :], bases[:, :], limit_b[0:1, :], None, ALU.max))
                dve.wait_ge(s_lob, 16)
                then(nc.vector.tensor_scalar(lo_b, lo_b, -1.0, limit_b, ALU.mult, ALU.add))
                then(nc.vector.tensor_scalar(lo_b, lo_b, 0.0, None, ALU.max))
                by_group = relT[:, :].rearrange("p (g t) -> p g t", t=TG)
                then(nc.vector.tensor_tensor(by_group, by_group, lo_b.unsqueeze(2).broadcast_to([P, GROUPS, TG]),
                                             ALU.subtract))
                first = ulist_i[:, 0:1]
                then(nc.vector.tensor_copy(first, unit_no[:, 0:1]))
                then(nc.vector.tensor_scalar(first, first, SUB.bit_length() - 1, None, ALU.arith_shift_right))
                then(nc.vector.tensor_copy(digit, first))
                then(nc.vector.scalar_tensor_tensor(out=digit, in0=digit, scalar=-float(SUB), in1=unit_no[:, 0:1],
                                                    op0=ALU.mult, op1=ALU.add))
                for k in range(P // PER):
                    if k:
                        dve.wait_ge(s_relP, k)
                    nc.vector.tensor_tensor(select[:, :].rearrange("p (u d) -> p u d", d=SUB),
                                            ident[:, k * PER:(k + 1) * PER].unsqueeze(2).broadcast_to([P, PER, SUB]),
                                            ident[:, k * PER:k * PER + 1].unsqueeze(2).broadcast_to([P, PER, SUB]),
                                            ALU.subtract).then_inc(s_relm, 1)
                dve.wait_ge(s_ugot, 16 * UC * UT)
                keys = gathered.rearrange("p (t n) -> p t n", n=2 * P)[:, :, 0:P]
                nc.vector.tensor_tensor(keys, keys, unit_shift[:, :, :].rearrange("p c i -> p (c i)").unsqueeze(2)
                                        .broadcast_to([P, UC * UT, P]), ALU.subtract).then_inc(s_ushift, 1)
                dve.wait_ge(s_relP, P // PER)
                K = P // PER
                nc.vector.tensor_scalar(relcol[:, :].rearrange("p (c k) -> p k c", k=K),
                                        ps_misc[:, 0:K * UC].rearrange("p (k c) -> p k c", k=K), float(SUB), digit,
                                        ALU.mult, ALU.add).then_inc(s_relC, 1)
                nc.vector.tensor_scalar(dbases[:, :].rearrange("p (c k) -> p k c", k=K),
                                        ps_misc[0:1, K * UC:2 * K * UC].rearrange("p (k c) -> p k c", k=K), float(SUB), None,
                                        ALU.mult).then_inc(s_relC, 1)
                dve.wait_ge(s_relC, 2)
                dve.wait_ge(s_w, 16 * 7)
                nc.vector.tensor_tensor(brz[:, :], bih[:, 0:2], bhh[:, 0:2], ALU.add).then_inc(s_dve, 1)
                done[0] += 1

                def rows_rest(u, k):
                    dve.wait_ge(s_hi, u + 1)
                    wait_past(dve, s_rC, u)
                    nc.vector.tensor_tensor(rest.rearrange("p (j n) -> p j n", j=CJ),
                                            ps_rows[0:CP, :].rearrange("p (j n) -> p j n", j=CJ), part_of(k, 0),
                                            ALU.subtract).then_inc(s_rest, 1)

                def rows_lo(u, k):
                    dve.wait_ge(s_mid, u + 1)
                    nc.vector.tensor_tensor(part_of(k, 2), rest.rearrange("p (j n) -> p j n", j=CJ),
                                            part_of(k, 1), ALU.subtract).then_inc(s_rC, 1)

                def moments(it, k):
                    c = it * SLOTS + k
                    dve.wait_ge(s_xload[k], (it + 1) * 16)
                    for j in range(CJ):
                        t = nc.vector.bn_stats(stats[:, j, :], xrow[:, k, j * P:(j + 1) * P])
                    t.then_inc(s_stats, 1)
                    dve.wait_ge(s_stats, c * 2 + 1)
                    dve.sem_inc(s_passed, 1)
                    for j in range(CJ):
                        t = nc.vector.bn_aggr(mv[:, j, :], stats[:, j, :])
                    t.then_inc(s_var, 1)

                def norm_step(it, k, first, following):
                    c = it * SLOTS + k
                    if first:
                        moments(0, 0)
                    dve.wait_ge(s_var, c + 1)
                    dve.wait_ge(s_std, c + 1)
                    nc.vector.reciprocal(rstd[:, :], rstd[:, :]).then_inc(s_stats, 1)
                    dve.wait_ge(s_stats, c * 2 + 2)
                    wait_past(dve, s_lnT, c)
                    for j in range(CJ):
                        t = nc.vector.tensor_scalar(xn[:, j * P:(j + 1) * P], xrow[:, k, j * P:(j + 1) * P],
                                                    mv[:, j, 0:1], rstd[:, j:j + 1], ALU.subtract, ALU.mult)
                    t.then_inc(s_xn, 1)
                    dve.wait_ge(s_xn, c + 1)
                    dve.sem_inc(s_xused, 1)
                    if following:
                        moments(*following)
                    if not first:
                        rows_rest(c - 1, (k - 1) % SLOTS)
                        rows_lo(c - 1, (k - 1) % SLOTS)

                norm_steps(dve, norm_step)
                rows_rest(CHUNKS - 1, SLOTS - 1)
                rows_lo(CHUNKS - 1, SLOTS - 1)

                dve.wait_ge(s_combC, 1)
                wide = dve.value_load(wide_i[0:1, 0:1], min_val=0, max_val=1)

                def group_onehot(it, u, k):
                    dve.wait_ge(s_sum, u * SLOTS + (k + 1))
                    nc.vector.tensor_tensor(
                        onehot[:, k, :].rearrange("p (t n) -> p t n", t=TG),
                        iota_b[:, :].unsqueeze(1).broadcast_to([P, TG, WIN]),
                        relT[:, bass.ds((it * SLOTS + k) * TG, TG)].unsqueeze(2).broadcast_to([P, TG, WIN]),
                        ALU.is_equal).then_inc(s_oh, 1)

                def group_add(it, u, k):
                    n = u * SLOTS + k
                    base = dve.value_load(bases[0:1, bass.ds(it * SLOTS + k, 1)], min_val=0, max_val=NODES - 1)
                    dve.wait_ge(s_sum, n + (SLOTS + 1))
                    dve.wait_ge(s_taken, n + 2)
                    at = aggT[:, bass.ds(base, WIN)]
                    nc.vector.tensor_tensor(at, at, sums[BANK[k]][:, 0:WIN], ALU.add).then_inc(s_taken, 1)

                def dense_add(j, w, groups):
                    base = dve.value_load(dbases[0:1, bass.ds(j, 1)], min_val=0, max_val=STRIPS * SUB)
                    dve.wait_ge(s_taken, groups + 2)
                    dve.wait_ge(s_dT, w + 1)
                    at = aggT[:, bass.ds(base, P)]
                    nc.vector.tensor_tensor(at, at, ps_denseT, ALU.add).then_inc(s_dadd, 1)
                    dve.wait_ge(s_dadd, w + 1)

                def dense_sum(bank, w):
                    dve.wait_ge(s_used[PIECES - 1], w + 1)
                    nc.vector.tensor_copy(dsum[:, :], bank[:, 2 * P:3 * P]).then_inc(s_dpart, 1)
                    for part in (1, 0):
                        dve.wait_ge(s_dpart, w * 2 + (2 - part))
                        nc.vector.tensor_tensor(dsum[:, :], dsum[:, :], bank[:, part * P:(part + 1) * P],
                                                ALU.add).then_inc(s_dpart if part else s_dcopy, 1)

                def make_select(j):
                    nc.vector.tensor_scalar(select[:, :], iota_b[:, :], relcol[:, bass.ds(j, 1)], None,
                                            ALU.is_equal).then_inc(s_sel, 1)

                def slow_groups(layer):
                    with dve.Fori(0, GROUPS) as g:
                        nc.vector.tensor_copy(shifted[:, :], dstT[:, bass.ds(g * TG, TG)]).then_inc(s_sh, 1)
                        with dve.Fori(0, SWINS) as w:
                            m = (g + layer * GROUPS) * SWINS + w
                            dve.wait_ge(s_sh, m + (g + layer * GROUPS) + 1)
                            nc.vector.tensor_tensor(
                                onehot_slow, iota_s[:, :].unsqueeze(1).broadcast_to([P, TG, SWIN]),
                                shifted[:, :].unsqueeze(2).broadcast_to([P, TG, SWIN]),
                                ALU.is_equal).then_inc(s_slow_oh, 1)
                            dve.wait_ge(s_slow_oh, m + 1)
                            nc.vector.tensor_scalar(shifted[:, :], shifted[:, :], float(SWIN), None,
                                                    ALU.subtract).then_inc(s_sh, 1)
                            dve.wait_ge(s_slow_sum, m + 1)
                            at = aggT[:, bass.ds(w * SWIN, SWIN)]
                            nc.vector.tensor_tensor(at, at, sums[0][:, 0:SWIN], ALU.add).then_inc(s_slow_add, 1)
                            dve.wait_ge(s_slow_add, m + 1)
                        dve.wait_ge(s_sh, (g + (layer * GROUPS + 1)) * (SWINS + 1))

                dve.wait_ge(s_uC, 2 * UC)
                dve.sem_inc(s_boh, 1)
                dve.sem_inc(s_bol, PAIRS)
                dve.sem_inc(s_boa, PAIRS // 2)
                nc.vector.tensor_copy(sw[:, 0, :], sloT[:, 0:PER * UT]).then_inc(s_sw, 1)
                nc.vector.tensor_copy(kw[:, 0, :], keyT[:, 0:PER * UT]).then_inc(s_kw, 1)
                with dve.Fori(0, DWINS // 2) as i:
                    for o in range(2):
                        w = i * 2 + o
                        dve.wait_ge(s_kw, w + 1)
                        dve.wait_ge(s_sw, w + 1)
                        for m in range(PAIRS):
                            if m == PAIRS // 2:
                                dve.wait_ge(s_bol, w * (PAIRS // 2) + PAIRS)
                                dve.wait_ge(s_boa, w * (PAIRS // 2) + PAIRS // 2)
                                nc.vector.tensor_copy(sw[:, 1 - o, :], sloT[:, bass.ds((w + 1) * (PER * UT), PER * UT)]
                                                      ).then_inc(s_sw, 1)
                                dve.wait_ge(s_boh, w * PAIRS + 1)
                                nc.vector.tensor_copy(kw[:, 1 - o, :], keyT[:, bass.ds((w + 1) * (PER * UT), PER * UT)]
                                                      ).then_inc(s_kw, 1)
                            if m % 2 == 0:
                                dve.wait_ge(s_bsum, w * PAIRS + (m + 2))
                                for t in range(ON_VECTOR):
                                    at = m * 2 * UT + t
                                    nc.vector.tensor_scalar(olv[:, m // 2 % 2, t, :], iota_b[:, :], sw[:, o, at:at + 1],
                                                            None, ALU.is_equal)
                            else:
                                dve.wait_ge(s_bsum, w * PAIRS + (m + 1))
                            for t in range(2 * UT):
                                ins = nc.vector.tensor_scalar(ohv[:, m % OB, t, :], iota_w,
                                                              kw[:, o, m * 2 * UT + t:m * 2 * UT + t + 1], None, ALU.is_equal)
                            ins.then_inc(s_boh, 1)
                dve.wait_ge(s_aS, 16 * DWINS)
                skip, kept = load_skip(dve)
                last, more = load_last(dve)
                for layer in range(LAYERS):
                    nc.vector.memset(aggT[:, :], 0.0).then_inc(s_zero, 1)
                    dve.wait_ge(s_zero, layer + 1)
                    with dve.If(wide):
                        slow_groups(layer)
                    with dve.Else():
                        past = kept * layer if layer else 0

                        def make_onehot(i, k):
                            i, k = i + k // SLOTS, k % SLOTS
                            group_onehot(iteration(skip, i), past + i, k)

                        def group(i, k):
                            make_onehot(i, k + 1)
                            group_add(iteration(skip, i), past + i, k)

                        def dense_step(d, rate):
                            body, iters, at_w, at_i = rate
                            if isinstance(d, int):
                                make_select(0)
                            for s in range(iters * SLOTS):
                                i, k = d * iters + (at_i + s // SLOTS), s % SLOTS
                                group(i, k)
                                for what, a in window_steps(s, rate):
                                    j = d * body + (at_w + a)
                                    w = d * body + (at_w + a + layer * DWINS)
                                    if what == "sum":
                                        dense_sum(dense_bank(a, rate), w)
                                    elif a >= 0 or not isinstance(d, int):
                                        dense_add(j, w, (past + i) * SLOTS + (k + 1))
                                        make_select(d * body + (at_w + a + 1))

                        make_onehot(0, 0)
                        dense_loops(dve, dense_step)
                        dense_add(DWINS - 1, (layer + 1) * DWINS - 1, (past + DITER) * SLOTS)
                        with dve.If(more):
                            with dve.Fori(DITER, last) as i:
                                for k in range(SLOTS):
                                    group(i, k)
                        for k in range(SLOTS):
                            if k < SLOTS - 1:
                                group(last, k)
                            else:
                                group_add(iteration(skip, last), past + last, k)
                        dve.wait_ge(s_taken, (past + kept) * SLOTS + 2)
                        dve.sem_inc(s_passed, 1)
                    dve.sem_inc(s_agg, 1)

                    def add_rows(it, k, u):
                        dve.wait_ge(s_rT, u + 1)
                        dve.wait_ge(s_xload[k], (it + (CITER + 1)) * 16)
                        dve.wait_ge(s_rS[k], (it + LAYERS * CITER) * 16)
                        nc.vector.tensor_tensor(hrow_f[:, k, 0:CJ * P], ps_rows[0:CP, :], xrow[:, k, :],
                                                ALU.add).then_inc(s_rC, 1)
                        dve.wait_ge(s_rC, u + 1)
                        dve.sem_inc(s_rest, 1)
                        dve.sem_inc(s_xused, 1)

                    def step(it, k, first):
                        c = it * SLOTS + k
                        v = c + layer * CHUNKS
                        h = hs[:, k, :]
                        before = (k - 1) % SLOTS
                        dve.wait_ge(s_n, v + 1)
                        dve.wait_ge(s_rzread, v + 1)
                        wait_past(dve, s_cand, v)
                        nc.vector.scalar_tensor_tensor(out=npre, in0=ps_hn[:, 0:CH], scalar=bhh[:, 2:3],
                                                       in1=gr, op0=ALU.add, op1=ALU.mult).then_inc(s_t1, 1)
                        dve.wait_ge(s_t1, v + 1)
                        nc.vector.tensor_tensor(npre, npre, ps_in[:, 0:CH], ALU.add).then_inc(s_nread, 1)
                        if not first:
                            if layer == LAYERS - 1:
                                add_rows(it - (k == 0), before, v + (CHUNKS - 1))
                            else:
                                rows_rest(v + (CHUNKS - 1), before)
                        dve.wait_ge(s_cand, v + 1)
                        nc.vector.tensor_tensor(diff, h, cand, ALU.subtract).then_inc(s_d, 1)
                        dve.wait_ge(s_d, v * 2 + 1)
                        nc.vector.tensor_tensor(diff, diff, gz, ALU.mult).then_inc(s_d, 1)
                        dve.wait_ge(s_d, v * 2 + 2)
                        nc.vector.tensor_tensor(h, diff, cand, ALU.add).then_inc(s_h0, 1)
                        dve.wait_ge(s_h0, v + (CHUNKS + 1))
                        if not first and layer < LAYERS - 1:
                            rows_lo(v + (CHUNKS - 1), before)

                    steps(dve, CITER, step)
                    if layer == LAYERS - 1:
                        add_rows(CITER - 1, SLOTS - 1, (layer + 2) * CHUNKS - 1)
                    else:
                        rows_rest((layer + 2) * CHUNKS - 1, SLOTS - 1)
                        rows_lo((layer + 2) * CHUNKS - 1, SLOTS - 1)


def kernel(x, src, dst, L0_gnn_lin_w, L0_gnn_lin_b, L0_gnn_weight, L0_gnn_w_ih, L0_gnn_w_hh, L0_gnn_b_ih, L0_gnn_b_hh):
    import numpy as np
    import concourse.bacc as bacc
    from concourse import mybir as mb
    from concourse.bass_utils import run_bass_kernel_spmd

    arrays = {
        "x": np.asarray(x), "src": np.asarray(src), "dst": np.asarray(dst),
        "lin_wT": np.asarray(L0_gnn_lin_w).T, "lin_b": np.asarray(L0_gnn_lin_b),
        "weightT": np.asarray(L0_gnn_weight).transpose(0, 2, 1), "w_ihT": np.asarray(L0_gnn_w_ih).T,
        "w_hhT": np.asarray(L0_gnn_w_hh).T, "b_ih": np.asarray(L0_gnn_b_ih), "b_hh": np.asarray(L0_gnn_b_hh),
    }
    arrays = {f"in_{k}": np.ascontiguousarray(v) for k, v in arrays.items()}
    nc = bacc.Bacc("TRN2", target_bir_lowering=False, num_devices=1)
    args = [nc.dram_tensor(k, v.shape, mb.dt.from_np(v.dtype), kind="ExternalInput").ap() for k, v in arrays.items()]
    shape = arrays["in_x"].shape
    out = nc.dram_tensor("out", shape, mb.dt.float32, kind="ExternalOutput").ap()
    build(nc, *args, out, NODES=shape[0], EDGES=arrays["in_src"].shape[0], LAYERS=arrays["in_weightT"].shape[0])
    r = run_bass_kernel_spmd(nc, [arrays], core_ids=[0])
    return r.results[0]["out"]
```
